# Optimizing a Trainium2 kernel written in Bass

```python
import numpy as np
import jax
import jax.numpy as jnp

def _softmax(x, axis=-1):
    return jax.nn.softmax(x, axis=axis)

def _gelu(x):
    return jax.nn.gelu(x, approximate=True)

def _silu(x):
    return jax.nn.silu(x)

def _sigmoid(x):
    return jax.nn.sigmoid(x)

def _layernorm(x, axis=-1, eps=1e-05):
    m = jnp.mean(x, axis=axis, keepdims=True)
    v = jnp.var(x, axis=axis, keepdims=True)
    return (x - m) / jnp.sqrt(v + eps)

def _scatter_add(tgt, idx, src, axis=0):
    return tgt.at[idx].add(src)

def _segment_sum(src, seg, n):
    return jax.ops.segment_sum(src, seg, n)
kernel_name = 'mk_sandwich_d4_jaxref_r8_60c9ce'

def setup_inputs(seed: int=0):
    np.random.seed(seed)
    _w = jnp.asarray

    def _L0_attn_setup():
        import jax, jax.numpy as jnp
        import numpy as np
        EMBED_DIM = 128
        K_DIM = 128
        MAX_SEQ_LEN = 256
        key = jax.random.key(seed)
        ks = jax.random.split(key, 9)
        s = 0.02
        x = jax.random.normal(ks[0], (4, 256, EMBED_DIM), dtype=jnp.float32)
        wq = jax.random.normal(ks[1], (EMBED_DIM, K_DIM), dtype=jnp.float32) * s
        bq = jnp.zeros((K_DIM,), dtype=jnp.float32)
        wk = jax.random.normal(ks[2], (EMBED_DIM, K_DIM), dtype=jnp.float32) * s
        bk = jnp.zeros((K_DIM,), dtype=jnp.float32)
        wv = jax.random.normal(ks[3], (EMBED_DIM, K_DIM), dtype=jnp.float32) * s
        bv = jnp.zeros((K_DIM,), dtype=jnp.float32)
        wo = jax.random.normal(ks[4], (K_DIM, EMBED_DIM), dtype=jnp.float32) * s
        bo = jnp.zeros((EMBED_DIM,), dtype=jnp.float32)
        return {'x': x, 'wq': wq, 'bq': bq, 'wk': wk, 'bk': bk, 'wv': wv, 'bv': bv, 'wo': wo, 'bo': bo}
    _L0_attn_in = _L0_attn_setup()

    def _L0_ffn_setup():
        import jax, jax.numpy as jnp
        import numpy as np
        DIM = 128
        HIDDEN = 384
        SCALE = 1.0 / 127.0

        def _dequant(w_int, dtype):
            return w_int.astype(dtype) * jnp.asarray(SCALE, dtype)
        key = jax.random.key(seed)
        k_x, k_g, k_u, k_d = jax.random.split(key, 4)
        x = jax.random.normal(k_x, (4, 256, DIM), dtype=jnp.float32)
        w_gate = jax.random.randint(k_g, (HIDDEN, DIM), -127, 128, dtype=jnp.int32)
        w_up = jax.random.randint(k_u, (HIDDEN, DIM), -127, 128, dtype=jnp.int32)
        w_down = jax.random.randint(k_d, (DIM, HIDDEN), -127, 128, dtype=jnp.int32)
        return {'x': x, 'w_gate': w_gate, 'w_up': w_up, 'w_down': w_down}
    _L0_ffn_in = _L0_ffn_setup()

    def _L1_attn_setup():
        import jax, jax.numpy as jnp
        import numpy as np
        B, N, DIM = (4, 512, 128)
        H, M = (16, 64)
        HD = DIM // H

        def iterative_inv(mat, n_iter=6):
            m = mat.shape[-1]
            I = jnp.eye(m, dtype=mat.dtype)
            K = mat
            denom = jnp.max(jnp.sum(K, axis=-2), axis=-1)[:, :, None, None]
            V = jnp.swapaxes(K, -1, -2) / denom
            for _ in range(n_iter):
                KV = jnp.matmul(K, V)
                V = jnp.matmul(0.25 * V, 13 * I - jnp.matmul(KV, 15 * I - jnp.matmul(KV, 7 * I - KV)))
            return V

        def _reference_tuple_inner(x, w_qkv, w_proj):
            b, n, c = x.shape
            qkv = (x @ w_qkv).reshape(b, n, 3, H, HD)
            qkv = jnp.transpose(qkv, (2, 0, 3, 1, 4))
            Q, K, V = (qkv[0], qkv[1], qkv[2])
            Q = Q / jnp.asarray(HD ** 0.5, dtype=Q.dtype)
            Q_l = Q.reshape(b, H, M, n // M, HD).mean(axis=-2)
            K_l = K.reshape(b, H, M, n // M, HD).mean(axis=-2)
            kernel1 = jax.nn.softmax(jnp.einsum('bhnd,bhmd->bhnm', Q, K_l), axis=-1)
            kernel2 = jax.nn.softmax(jnp.einsum('bhmd,bhkd->bhmk', Q_l, K_l), axis=-1)
            kernel3 = jax.nn.softmax(jnp.einsum('bhmd,bhnd->bhmn', Q_l, K), axis=-1)
            SV = jnp.matmul(jnp.matmul(kernel1, iterative_inv(kernel2)), jnp.matmul(kernel3, V))
            SV = jnp.transpose(SV, (0, 2, 1, 3)).reshape(b, n, c)
            out = SV @ w_proj
            return (out, SV)
        key = jax.random.key(seed)
        k1, k2, k3 = jax.random.split(key, 3)
        x = jax.random.normal(k1, (B, N, DIM), dtype=jnp.float32)
        w_qkv = jax.random.normal(k2, (DIM, 3 * DIM), dtype=jnp.float32) * 0.02
        w_proj = jax.random.normal(k3, (DIM, DIM), dtype=jnp.float32) * 0.02
        return {'x': x, 'w_qkv': w_qkv, 'w_proj': w_proj}
    _L1_attn_in = _L1_attn_setup()

    def _L1_ffn_setup():
        import jax, jax.numpy as jnp
        import numpy as np
        B, S, D = (4, 64, 128)
        E, K, H = (64, 8, 32)
        ES, HS = (2, 256)
        key = jax.random.key(seed)
        ks = jax.random.split(key, 8)
        scale = 0.02
        rn = lambda k, shape, s: jax.random.normal(k, shape, jnp.float32) * s
        return {'x': rn(ks[0], (B, S, D), 1.0), 'router_w': rn(ks[1], (D, E), scale), 'router_b': jnp.zeros((E,), jnp.float32), 'w1': rn(ks[2], (E, D, H), scale), 'b1': jnp.zeros((E, H), jnp.float32), 'w2': rn(ks[3], (E, H, D), scale), 'b2': jnp.zeros((E, D), jnp.float32), 'sw1': rn(ks[4], (ES, D, HS), scale), 'sb1': jnp.zeros((ES, HS), jnp.float32), 'sw2': rn(ks[5], (ES, HS, D), scale), 'sb2': jnp.zeros((ES, D), jnp.float32)}
    _L1_ffn_in = _L1_ffn_setup()

    def _L2_attn_setup():
        import jax, jax.numpy as jnp
        import numpy as np
        B, T, D, H = (4, 256, 128, 16)
        HD = D // H
        ROPE_BASE = 10000.0

        def rotate_half(x):
            x1 = x[..., ::2]
            x2 = x[..., 1::2]
            return jnp.stack((-x2, x1), axis=-1).reshape(x.shape)

        def rope_tables(seq_len, dim, dtype=jnp.float32):
            inv = 1.0 / ROPE_BASE ** (jnp.arange(0, dim, 2, dtype=jnp.float32) / dim)
            t = jnp.arange(seq_len, dtype=jnp.float32)
            freqs = jnp.einsum('i,j->ij', t, inv)
            emb = jnp.concatenate((freqs, freqs), axis=-1)
            return (jnp.cos(emb).astype(dtype)[None, None], jnp.sin(emb).astype(dtype)[None, None])
        key = jax.random.key(seed)
        ks = jax.random.split(key, 9)
        s = 0.02
        return {'x': jax.random.normal(ks[0], (B, T, D), jnp.float32), 'Wq': jax.random.normal(ks[1], (D, D), jnp.float32) * s, 'bq': jnp.zeros((D,), jnp.float32), 'Wk': jax.random.normal(ks[2], (D, D), jnp.float32) * s, 'bk': jnp.zeros((D,), jnp.float32), 'Wv': jax.random.normal(ks[3], (D, D), jnp.float32) * s, 'bv': jnp.zeros((D,), jnp.float32), 'Wo': jax.random.normal(ks[4], (D, D), jnp.float32) * s, 'bo': jnp.zeros((D,), jnp.float32)}
    _L2_attn_in = _L2_attn_setup()

    def _L2_ffn_setup():
        import jax, jax.numpy as jnp
        import numpy as np
        B, S, H = (1, 256, 128)
        E = 16
        I = 96
        TOPK = 4
        G = 4
        TOPK_G = 2
        SCALE = 2.5
        N_SHARED = 1

        def _route(x, gate_w, gate_bias):
            n = x.shape[0]
            logits = jnp.einsum('nh,eh->ne', x.astype(jnp.float32), gate_w)
            scores = jax.nn.sigmoid(logits)
            sb = scores + gate_bias
            gs = sb.reshape(n, G, E // G)
            group_scores = jnp.sum(jax.lax.top_k(gs, 2)[0], axis=-1)
            _, gidx = jax.lax.top_k(group_scores, TOPK_G)
            gmask = jnp.sum(jax.nn.one_hot(gidx, G, dtype=sb.dtype), axis=1)
            emask = jnp.repeat(gmask, E // G, axis=-1)
            masked = jnp.where(emask > 0, sb, -jnp.inf)
            _, tidx = jax.lax.top_k(masked, TOPK)
            w = jnp.take_along_axis(scores, tidx, axis=1)
            w = w / (jnp.sum(w, axis=-1, keepdims=True) + 1e-20)
            return (tidx, w * SCALE)
        key = jax.random.key(seed)
        ks = jax.random.split(key, 9)

        def rn(k, shape, scale=0.02):
            return jax.random.normal(k, shape, dtype=jnp.float32) * scale
        return dict(hidden_states=jax.random.normal(ks[0], (B, S, H), dtype=jnp.float32), gate_w=rn(ks[1], (E, H)), gate_bias=jax.random.normal(ks[2], (E,), dtype=jnp.float32) * 0.1, w1=rn(ks[3], (E, I, H)), w2=rn(ks[4], (E, H, I)), w3=rn(ks[5], (E, I, H)), ws1=rn(ks[6], (I * N_SHARED, H)), ws2=rn(ks[7], (H, I * N_SHARED)), ws3=rn(ks[8], (I * N_SHARED, H)))
    _L2_ffn_in = _L2_ffn_setup()

    def _L3_attn_setup():
        import jax, jax.numpy as jnp
        import numpy as np
        import math
        D_MODEL = 128
        N_HEADS = 16
        HEAD_DIM = D_MODEL // N_HEADS

        def rotary_embedding(dim, seq_len):
            inv_freq = 1.0 / 10000.0 ** (jnp.arange(0, dim, 2, dtype=jnp.float32) / dim)
            t = jnp.arange(seq_len, dtype=jnp.float32)
            freqs = t[:, None] * inv_freq[None, :]
            return jnp.concatenate((freqs, freqs), axis=-1)

        def apply_rope(x, rope):
            x1 = x[..., ::2]
            x2 = x[..., 1::2]
            ang = rope[..., ::2]
            c, s = (jnp.cos(ang), jnp.sin(ang))
            o1 = x1 * c - x2 * s
            o2 = x1 * s + x2 * c
            return jnp.stack((o1, o2), axis=-1).reshape(x.shape)
        key = jax.random.key(seed)
        ks = jax.random.split(key, 9)
        d = D_MODEL
        sc = 1.0 / math.sqrt(d)
        return {'x': jax.random.normal(ks[0], (2, 256, d), dtype=jnp.float32), 'Wq': jax.random.normal(ks[1], (d, d), dtype=jnp.float32) * sc, 'bq': jax.random.normal(ks[2], (d,), dtype=jnp.float32) * 0.02, 'Wk': jax.random.normal(ks[3], (d, d), dtype=jnp.float32) * sc, 'bk': jax.random.normal(ks[4], (d,), dtype=jnp.float32) * 0.02, 'Wv': jax.random.normal(ks[5], (d, d), dtype=jnp.float32) * sc, 'bv': jax.random.normal(ks[6], (d,), dtype=jnp.float32) * 0.02, 'Wo': jax.random.normal(ks[7], (d, d), dtype=jnp.float32) * sc, 'bo': jax.random.normal(ks[8], (d,), dtype=jnp.float32) * 0.02}
    _L3_attn_in = _L3_attn_setup()

    def _L3_ffn_setup():
        import jax, jax.numpy as jnp
        import numpy as np
        D_IN, D_HID = (128, 512)

        def _ternary(key, shape):
            return jax.random.randint(key, shape, -1, 2).astype(jnp.float32)

        def _tlin(x, w, s):
            return jnp.einsum('bsi,oi->bso', x, w) * s
        key = jax.random.key(seed)
        ks = jax.random.split(key, 12)
        inv = lambda fan: 1.0 / np.sqrt(fan).astype(np.float32)
        return {'x': jax.random.normal(ks[0], (4, 256, D_IN), dtype=jnp.float32), 'w1_w': _ternary(ks[1], (D_HID, D_IN)), 'w1_s': jax.random.uniform(ks[2], (D_HID,), dtype=jnp.float32) * inv(D_IN), 'w2_w': _ternary(ks[3], (D_HID, D_IN)), 'w2_s': jax.random.uniform(ks[4], (D_HID,), dtype=jnp.float32) * inv(D_IN), 'h1_w': _ternary(ks[5], (D_HID, D_HID)), 'h1_s': jax.random.uniform(ks[6], (D_HID,), dtype=jnp.float32) * inv(D_HID), 'h2_w': _ternary(ks[7], (D_HID, D_HID)), 'h2_s': jax.random.uniform(ks[8], (D_HID,), dtype=jnp.float32) * inv(D_HID), 'w3_w': _ternary(ks[9], (D_IN, D_HID)), 'w3_s': jax.random.uniform(ks[10], (D_IN,), dtype=jnp.float32) * inv(D_HID)}
    _L3_ffn_in = _L3_ffn_setup()
    _d = {'L0_attn_x': _L0_attn_in['x'], 'L0_attn_wq': _L0_attn_in['wq'], 'L0_attn_bq': _L0_attn_in['bq'], 'L0_attn_wk': _L0_attn_in['wk'], 'L0_attn_bk': _L0_attn_in['bk'], 'L0_attn_wv': _L0_attn_in['wv'], 'L0_attn_bv': _L0_attn_in['bv'], 'L0_attn_wo': _L0_attn_in['wo'], 'L0_attn_bo': _L0_attn_in['bo'], 'L0_ffn_w_gate': _L0_ffn_in['w_gate'], 'L0_ffn_w_up': _L0_ffn_in['w_up'], 'L0_ffn_w_down': _L0_ffn_in['w_down'], 'L1_attn_w_qkv': _L1_attn_in['w_qkv'], 'L1_attn_w_proj': _L1_attn_in['w_proj'], 'L1_ffn_router_w': _L1_ffn_in['router_w'], 'L1_ffn_router_b': _L1_ffn_in['router_b'], 'L1_ffn_w1': _L1_ffn_in['w1'], 'L1_ffn_b1': _L1_ffn_in['b1'], 'L1_ffn_w2': _L1_ffn_in['w2'], 'L1_ffn_b2': _L1_ffn_in['b2'], 'L1_ffn_sw1': _L1_ffn_in['sw1'], 'L1_ffn_sb1': _L1_ffn_in['sb1'], 'L1_ffn_sw2': _L1_ffn_in['sw2'], 'L1_ffn_sb2': _L1_ffn_in['sb2'], 'L2_attn_Wq': _L2_attn_in['Wq'], 'L2_attn_bq': _L2_attn_in['bq'], 'L2_attn_Wk': _L2_attn_in['Wk'], 'L2_attn_bk': _L2_attn_in['bk'], 'L2_attn_Wv': _L2_attn_in['Wv'], 'L2_attn_bv': _L2_attn_in['bv'], 'L2_attn_Wo': _L2_attn_in['Wo'], 'L2_attn_bo': _L2_attn_in['bo'], 'L2_ffn_gate_w': _L2_ffn_in['gate_w'], 'L2_ffn_gate_bias': _L2_ffn_in['gate_bias'], 'L2_ffn_w1': _L2_ffn_in['w1'], 'L2_ffn_w2': _L2_ffn_in['w2'], 'L2_ffn_w3': _L2_ffn_in['w3'], 'L2_ffn_ws1': _L2_ffn_in['ws1'], 'L2_ffn_ws2': _L2_ffn_in['ws2'], 'L2_ffn_ws3': _L2_ffn_in['ws3'], 'L3_attn_Wq': _L3_attn_in['Wq'], 'L3_attn_bq': _L3_attn_in['bq'], 'L3_attn_Wk': _L3_attn_in['Wk'], 'L3_attn_bk': _L3_attn_in['bk'], 'L3_attn_Wv': _L3_attn_in['Wv'], 'L3_attn_bv': _L3_attn_in['bv'], 'L3_attn_Wo': _L3_attn_in['Wo'], 'L3_attn_bo': _L3_attn_in['bo'], 'L3_ffn_w1_w': _L3_ffn_in['w1_w'], 'L3_ffn_w1_s': _L3_ffn_in['w1_s'], 'L3_ffn_w2_w': _L3_ffn_in['w2_w'], 'L3_ffn_w2_s': _L3_ffn_in['w2_s'], 'L3_ffn_h1_w': _L3_ffn_in['h1_w'], 'L3_ffn_h1_s': _L3_ffn_in['h1_s'], 'L3_ffn_h2_w': _L3_ffn_in['h2_w'], 'L3_ffn_h2_s': _L3_ffn_in['h2_s'], 'L3_ffn_w3_w': _L3_ffn_in['w3_w'], 'L3_ffn_w3_s': _L3_ffn_in['w3_s']}
    _x0 = _d['L0_attn_x']
    _d['L0_attn_x'] = jax.random.normal(jax.random.fold_in(jax.random.key(seed), 1), (16, 256, 128), dtype=_x0.dtype)
    del _x0
    return _d

def reference(L0_attn_x, L0_attn_wq, L0_attn_bq, L0_attn_wk, L0_attn_bk, L0_attn_wv, L0_attn_bv, L0_attn_wo, L0_attn_bo, L0_ffn_w_gate, L0_ffn_w_up, L0_ffn_w_down, L1_attn_w_qkv, L1_attn_w_proj, L1_ffn_router_w, L1_ffn_router_b, L1_ffn_w1, L1_ffn_b1, L1_ffn_w2, L1_ffn_b2, L1_ffn_sw1, L1_ffn_sb1, L1_ffn_sw2, L1_ffn_sb2, L2_attn_Wq, L2_attn_bq, L2_attn_Wk, L2_attn_bk, L2_attn_Wv, L2_attn_bv, L2_attn_Wo, L2_attn_bo, L2_ffn_gate_w, L2_ffn_gate_bias, L2_ffn_w1, L2_ffn_w2, L2_ffn_w3, L2_ffn_ws1, L2_ffn_ws2, L2_ffn_ws3, L3_attn_Wq, L3_attn_bq, L3_attn_Wk, L3_attn_bk, L3_attn_Wv, L3_attn_bv, L3_attn_Wo, L3_attn_bo, L3_ffn_w1_w, L3_ffn_w1_s, L3_ffn_w2_w, L3_ffn_w2_s, L3_ffn_h1_w, L3_ffn_h1_s, L3_ffn_h2_w, L3_ffn_h2_s, L3_ffn_w3_w, L3_ffn_w3_s):

    def _L0_attn_ref(x, wq, bq, wk, bk, wv, bv, wo, bo):
        import jax, jax.numpy as jnp
        import numpy as np
        EMBED_DIM = 128
        K_DIM = 128
        MAX_SEQ_LEN = 256
        B, S, D = x.shape
        scale = jnp.asarray(K_DIM ** 0.5, x.dtype)
        Q = x @ wq + bq
        K = x @ wk + bk
        V = x @ wv + bv
        scores = jnp.einsum('bqk,bsk->bqs', Q, K) / scale
        row = jnp.arange(S)[:, None]
        col = jnp.arange(S)[None, :]
        mask = col <= row + 1
        scores = jnp.where(mask, jnp.asarray(-1000000000.0, scores.dtype), scores)
        attn = jax.nn.softmax(scores, axis=-1)
        out = jnp.einsum('bqs,bsk->bqk', attn, V)
        return out @ wo + bo

    def _L0_ffn_ref(x, w_gate, w_up, w_down):
        import jax, jax.numpy as jnp
        import numpy as np
        DIM = 128
        HIDDEN = 384
        SCALE = 1.0 / 127.0

        def _dequant(w_int, dtype):
            return w_int.astype(dtype) * jnp.asarray(SCALE, dtype)
        wg = _dequant(w_gate, x.dtype)
        wu = _dequant(w_up, x.dtype)
        wd = _dequant(w_down, x.dtype)
        gate = jnp.einsum('bsd,hd->bsh', x, wg)
        up = jnp.einsum('bsd,hd->bsh', x, wu)
        h = jax.nn.silu(gate) * up
        return jnp.einsum('bsh,dh->bsd', h, wd)

    def _L1_attn_ref(x, w_qkv, w_proj):
        import jax, jax.numpy as jnp
        import numpy as np
        B, N, DIM = (4, 512, 128)
        H, M = (16, 64)
        HD = DIM // H

        def iterative_inv(mat, n_iter=6):
            m = mat.shape[-1]
            I = jnp.eye(m, dtype=mat.dtype)
            K = mat
            denom = jnp.max(jnp.sum(K, axis=-2), axis=-1)[:, :, None, None]
            V = jnp.swapaxes(K, -1, -2) / denom
            for _ in range(n_iter):
                KV = jnp.matmul(K, V)
                V = jnp.matmul(0.25 * V, 13 * I - jnp.matmul(KV, 15 * I - jnp.matmul(KV, 7 * I - KV)))
            return V

        def _reference_tuple_inner(x, w_qkv, w_proj):
            b, n, c = x.shape
            qkv = (x @ w_qkv).reshape(b, n, 3, H, HD)
            qkv = jnp.transpose(qkv, (2, 0, 3, 1, 4))
            Q, K, V = (qkv[0], qkv[1], qkv[2])
            Q = Q / jnp.asarray(HD ** 0.5, dtype=Q.dtype)
            Q_l = Q.reshape(b, H, M, n // M, HD).mean(axis=-2)
            K_l = K.reshape(b, H, M, n // M, HD).mean(axis=-2)
            kernel1 = jax.nn.softmax(jnp.einsum('bhnd,bhmd->bhnm', Q, K_l), axis=-1)
            kernel2 = jax.nn.softmax(jnp.einsum('bhmd,bhkd->bhmk', Q_l, K_l), axis=-1)
            kernel3 = jax.nn.softmax(jnp.einsum('bhmd,bhnd->bhmn', Q_l, K), axis=-1)
            SV = jnp.matmul(jnp.matmul(kernel1, iterative_inv(kernel2)), jnp.matmul(kernel3, V))
            SV = jnp.transpose(SV, (0, 2, 1, 3)).reshape(b, n, c)
            out = SV @ w_proj
            return (out, SV)
        return _reference_tuple_inner(x, w_qkv, w_proj)[0]

    def _L1_ffn_ref(x, router_w, router_b, w1, b1, w2, b2, sw1, sb1, sw2, sb2):
        import jax, jax.numpy as jnp
        import numpy as np
        B, S, D = (4, 64, 128)
        E, K, H = (64, 8, 32)
        ES, HS = (2, 256)
        b_, s_, d_ = x.shape
        xf = x.reshape(-1, d_)
        probs = jax.nn.softmax(xf @ router_w + router_b, axis=-1)
        tw, ti = jax.lax.top_k(probs, K)
        tw = tw / jnp.sum(tw, axis=-1, keepdims=True)

        def body(acc, p):
            W1, B1, W2, B2, e = p
            h = jax.nn.silu(xf @ W1 + B1) @ W2 + B2
            cw = jnp.sum(jnp.where(ti == e, tw, 0.0), axis=-1)
            return (acc + cw[:, None] * h, None)
        routed, _ = jax.lax.scan(body, jnp.zeros_like(xf), (w1, b1, w2, b2, jnp.arange(w1.shape[0])))

        def shared_mlp(W1, B1, W2, B2):
            return jax.nn.silu(xf @ W1 + B1) @ W2 + B2
        shared = jnp.sum(jax.vmap(shared_mlp)(sw1, sb1, sw2, sb2), axis=0)
        return (routed + shared).reshape(b_, s_, d_)

    def _L2_attn_ref(x, Wq, bq, Wk, bk, Wv, bv, Wo, bo):
        import jax, jax.numpy as jnp
        import numpy as np
        B, T, D, H = (4, 256, 128, 16)
        HD = D // H
        ROPE_BASE = 10000.0

        def rotate_half(x):
            x1 = x[..., ::2]
            x2 = x[..., 1::2]
            return jnp.stack((-x2, x1), axis=-1).reshape(x.shape)

        def rope_tables(seq_len, dim, dtype=jnp.float32):
            inv = 1.0 / ROPE_BASE ** (jnp.arange(0, dim, 2, dtype=jnp.float32) / dim)
            t = jnp.arange(seq_len, dtype=jnp.float32)
            freqs = jnp.einsum('i,j->ij', t, inv)
            emb = jnp.concatenate((freqs, freqs), axis=-1)
            return (jnp.cos(emb).astype(dtype)[None, None], jnp.sin(emb).astype(dtype)[None, None])
        b, t, d = x.shape

        def proj(W, bias):
            return (x @ W.T + bias).reshape(b, t, H, HD).transpose(0, 2, 1, 3)
        q, k, v = (proj(Wq, bq), proj(Wk, bk), proj(Wv, bv))
        cos, sin = rope_tables(t, HD, x.dtype)
        q = q * cos + rotate_half(q) * sin
        k = k * cos + rotate_half(k) * sin
        scale = 1.0 / jnp.sqrt(jnp.asarray(HD, x.dtype))
        attn = jnp.einsum('bhqd,bhkd->bhqk', q, k) * scale
        attn = jax.nn.softmax(attn, axis=-1)
        out = jnp.einsum('bhqk,bhkd->bhqd', attn, v)
        out = out.transpose(0, 2, 1, 3).reshape(b, t, d)
        return out @ Wo.T + bo

    def _L2_ffn_ref(hidden_states, gate_w, gate_bias, w1, w2, w3, ws1, ws2, ws3):
        import jax, jax.numpy as jnp
        import numpy as np
        B, S, H = (1, 256, 128)
        E = 16
        I = 96
        TOPK = 4
        G = 4
        TOPK_G = 2
        SCALE = 2.5
        N_SHARED = 1

        def _route(x, gate_w, gate_bias):
            n = x.shape[0]
            logits = jnp.einsum('nh,eh->ne', x.astype(jnp.float32), gate_w)
            scores = jax.nn.sigmoid(logits)
            sb = scores + gate_bias
            gs = sb.reshape(n, G, E // G)
            group_scores = jnp.sum(jax.lax.top_k(gs, 2)[0], axis=-1)
            _, gidx = jax.lax.top_k(group_scores, TOPK_G)
            gmask = jnp.sum(jax.nn.one_hot(gidx, G, dtype=sb.dtype), axis=1)
            emask = jnp.repeat(gmask, E // G, axis=-1)
            masked = jnp.where(emask > 0, sb, -jnp.inf)
            _, tidx = jax.lax.top_k(masked, TOPK)
            w = jnp.take_along_axis(scores, tidx, axis=1)
            w = w / (jnp.sum(w, axis=-1, keepdims=True) + 1e-20)
            return (tidx, w * SCALE)
        b, s, h = hidden_states.shape
        x = hidden_states.reshape(-1, h)
        tidx, tw = _route(x, gate_w, gate_bias)
        n = x.shape[0]
        combine = jnp.zeros((n, E), x.dtype).at[jnp.arange(n)[:, None], tidx].add(tw)
        g = jnp.einsum('nh,eih->nei', x, w1)
        u = jnp.einsum('nh,eih->nei', x, w3)
        hact = jax.nn.silu(g) * u * combine[:, :, None]
        y = jnp.einsum('nei,ehi->nh', hact, w2)
        shared = jnp.einsum('ni,hi->nh', jax.nn.silu(x @ ws1.T) * (x @ ws3.T), ws2)
        return (y + shared).reshape(b, s, h)

    def _L3_attn_ref(x, Wq, bq, Wk, bk, Wv, bv, Wo, bo):
        import jax, jax.numpy as jnp
        import numpy as np
        import math
        D_MODEL = 128
        N_HEADS = 16
        HEAD_DIM = D_MODEL // N_HEADS

        def rotary_embedding(dim, seq_len):
            inv_freq = 1.0 / 10000.0 ** (jnp.arange(0, dim, 2, dtype=jnp.float32) / dim)
            t = jnp.arange(seq_len, dtype=jnp.float32)
            freqs = t[:, None] * inv_freq[None, :]
            return jnp.concatenate((freqs, freqs), axis=-1)

        def apply_rope(x, rope):
            x1 = x[..., ::2]
            x2 = x[..., 1::2]
            ang = rope[..., ::2]
            c, s = (jnp.cos(ang), jnp.sin(ang))
            o1 = x1 * c - x2 * s
            o2 = x1 * s + x2 * c
            return jnp.stack((o1, o2), axis=-1).reshape(x.shape)
        B, S, d = x.shape
        H, Dh = (N_HEADS, HEAD_DIM)
        q = (x @ Wq + bq).reshape(B, S, H, Dh).transpose(0, 2, 1, 3)
        k = (x @ Wk + bk).reshape(B, S, H, Dh).transpose(0, 2, 1, 3)
        v = (x @ Wv + bv).reshape(B, S, H, Dh).transpose(0, 2, 1, 3)
        rope = rotary_embedding(Dh, S)
        q = apply_rope(q, rope)
        k = apply_rope(k, rope)
        scores = jnp.einsum('bhqd,bhkd->bhqk', q, k) / math.sqrt(Dh)
        attn = jax.nn.softmax(scores, axis=-1)
        out = jnp.einsum('bhqk,bhkd->bhqd', attn, v)
        out = out.transpose(0, 2, 1, 3).reshape(B, S, d)
        return out @ Wo + bo

    def _L3_ffn_ref(x, w1_w, w1_s, w2_w, w2_s, h1_w, h1_s, h2_w, h2_s, w3_w, w3_s):
        import jax, jax.numpy as jnp
        import numpy as np
        D_IN, D_HID = (128, 512)

        def _ternary(key, shape):
            return jax.random.randint(key, shape, -1, 2).astype(jnp.float32)

        def _tlin(x, w, s):
            return jnp.einsum('bsi,oi->bso', x, w) * s
        h = jax.nn.silu(_tlin(x, w1_w, w1_s)) * _tlin(x, w2_w, w2_s)
        h = jax.nn.gelu(_tlin(h, h1_w, h1_s), approximate=False)
        h = jax.nn.gelu(_tlin(h, h2_w, h2_s), approximate=False)
        return _tlin(h, w3_w, w3_s)
    x = L0_attn_x
    x = x + _layernorm(_L0_attn_ref(_layernorm(x, axis=-1), L0_attn_wq, L0_attn_bq, L0_attn_wk, L0_attn_bk, L0_attn_wv, L0_attn_bv, L0_attn_wo, L0_attn_bo), axis=-1)
    x = x + _layernorm(_L0_ffn_ref(_layernorm(x, axis=-1), L0_ffn_w_gate, L0_ffn_w_up, L0_ffn_w_down), axis=-1)
    x = x + _layernorm(_L1_attn_ref(_layernorm(x, axis=-1), L1_attn_w_qkv, L1_attn_w_proj), axis=-1)
    x = x + _layernorm(_L1_ffn_ref(_layernorm(x, axis=-1), L1_ffn_router_w, L1_ffn_router_b, L1_ffn_w1, L1_ffn_b1, L1_ffn_w2, L1_ffn_b2, L1_ffn_sw1, L1_ffn_sb1, L1_ffn_sw2, L1_ffn_sb2), axis=-1)
    x = x + _layernorm(_L2_attn_ref(_layernorm(x, axis=-1), L2_attn_Wq, L2_attn_bq, L2_attn_Wk, L2_attn_bk, L2_attn_Wv, L2_attn_bv, L2_attn_Wo, L2_attn_bo), axis=-1)
    x = x + _layernorm(_L2_ffn_ref(_layernorm(x, axis=-1), L2_ffn_gate_w, L2_ffn_gate_bias, L2_ffn_w1, L2_ffn_w2, L2_ffn_w3, L2_ffn_ws1, L2_ffn_ws2, L2_ffn_ws3), axis=-1)
    x = x + _layernorm(_L3_attn_ref(_layernorm(x, axis=-1), L3_attn_Wq, L3_attn_bq, L3_attn_Wk, L3_attn_bk, L3_attn_Wv, L3_attn_bv, L3_attn_Wo, L3_attn_bo), axis=-1)
    x = x + _layernorm(_L3_ffn_ref(_layernorm(x, axis=-1), L3_ffn_w1_w, L3_ffn_w1_s, L3_ffn_w2_w, L3_ffn_w2_s, L3_ffn_h1_w, L3_ffn_h1_s, L3_ffn_h2_w, L3_ffn_h2_s, L3_ffn_w3_w, L3_ffn_w3_s), axis=-1)
    return x

_drawn_inputs = setup_inputs


def setup_inputs(seed=0):
    import zlib

    import numpy as np

    out = dict(_drawn_inputs(seed))
    spreads = {'L0_attn_bq': (0.0, 0.726),
     'L0_attn_bk': (0.0, 2.0),
     'L0_attn_bv': (0.0, 0.1),
     'L0_attn_bo': (0.0, 0.1),
     'L1_ffn_router_b': (0.0, 0.1),
     'L1_ffn_b1': (0.0, 0.453),
     'L1_ffn_b2': (0.0, 0.1),
     'L1_ffn_sb1': (0.0, 0.1),
     'L1_ffn_sb2': (0.0, 0.1),
     'L2_attn_bq': (0.0, 0.8),
     'L2_attn_bk': (0.0, 0.8),
     'L2_attn_bv': (0.0, 0.1),
     'L2_attn_bo': (0.0, 0.1)}
    factors = {'L0_attn_wq': 4.178,
     'L0_attn_wk': 3.999,
     'L2_attn_Wq': 8.0,
     'L2_attn_Wk': 8.0,
     'L3_attn_bq': 64.0,
     'L3_attn_bk': 64.0,
     'L3_attn_bv': 4.529,
     'L3_attn_bo': 4.994}
    for name, (base, spread) in spreads.items():
        noise = np.random.default_rng([zlib.crc32(name.encode()), seed]).standard_normal(out[name].shape)
        drawn = base * np.exp(spread * noise) if base else spread * noise
        out[name] = jnp.asarray(drawn.astype(out[name].dtype))
    for name, factor in factors.items():
        out[name] = (out[name] * factor).astype(out[name].dtype)
    return out
```

```python
import numpy as np
import concourse.bass as bass
from concourse import mybir
from contextlib import ExitStack

F32 = mybir.dt.float32
BF16 = mybir.dt.bfloat16
I32 = mybir.dt.int32
ALU = mybir.AluOpType
ACT = mybir.ActivationFunctionType
AX = mybir.AxisListType

D = 128
BATCHES, SEQ = 16, 256
TOKENS = BATCHES * SEQ
TILES = TOKENS // 128
EPS = 1e-5
FFN_TOKENS = 512
FFN_BLOCKS = TOKENS // FFN_TOKENS
FFN_TILES = FFN_TOKENS // 128
ATT_TILES = SEQ // 128
HEADS, HD = 16, 8


def wait(eng, sem, count):
    if not (isinstance(count, int) and count <= 0):
        eng.wait_ge(sem, count)


def wait_apart(eng, sem, count, passed):
    eng.wait_ge(sem, count)
    if not isinstance(count, int):
        eng.sem_inc(passed, 1)


class Chain:

    def __init__(self, eng, sem, n, per):
        self.eng, self.sem, self.n, self.per, self.j = eng, sem, n, per, 0

    def link(self, ins, passed=None):
        self.j += 1
        ins.then_inc(self.sem, 1)
        if passed is None:
            self.eng.wait_ge(self.sem, self.n * self.per + self.j)
        else:
            wait_apart(self.eng, self.sem, self.n * self.per + self.j, passed)

    def last(self, ins):
        self.j += 1
        assert self.j == self.per, (self.j, self.per)
        ins.then_inc(self.sem, 1)


def blocks(eng, count, body):
    body(0, 0, True, False)
    with eng.Fori(0, (count - 2) // 2) as i:
        body(2 * i + 1, 1, False, False)
        body(2 * i + 2, 0, False, False)
    body(count - 1, (count - 1) % 2, False, True)


class Core:

    def __init__(self, nc, ctx):
        self.nc, self.ctx = nc, ctx
        self.x = self.sbuf("x_all", [128, TILES + FFN_TILES, D], F32)
        self.half = self.sbuf("minus_half", [128, 4], F32)
        self.eps = self.sbuf("eps", [128, 4], F32)
        self.zero = self.sbuf("zero", [128, 1], F32)
        self.dve_passed = ctx.enter_context(nc.semaphore("dve_waits_passed"))
        self.sp_passed = ctx.enter_context(nc.semaphore("sp_waits_passed"))
        self.pe_passed = ctx.enter_context(nc.semaphore("pe_waits_passed"))

    def sbuf(self, name, shape, dt=F32):
        return self.ctx.enter_context(self.nc.sbuf_tensor(name, shape, dt))


class Stage:

    def __init__(self, nc, ctx, core, name):
        self.nc, self.ctx, self.name, self.sems = nc, ctx, name, []
        self.first, self.last = name == core.weights.stages[0], name == core.weights.stages[-1]

    def sbuf(self, name, shape, dt=F32):
        return self.ctx.enter_context(self.nc.sbuf_tensor(f"{self.name}_{name}", shape, dt))

    def bank(self, name, shape, dt=F32):
        return self.ctx.enter_context(self.nc.psum_tensor(f"{self.name}_{name}", shape, dt))

    def sem(self, name):
        self.sems.append(self.nc.alloc_semaphore(f"{self.name}_{name}"))
        return self.sems[-1]

    def clear(self):
        numbers = [s.num for s in self.sems]
        self.nc.clear_and_free_semaphores(self.sems)
        for num in numbers:
            self.nc.release_semaphore(self.nc.alloc_semaphore(f"{self.name}_used_{num}", num=num))


class Norms:

    def __init__(self, nc, core, stage, tiles):
        self.nc, self.core, self.tiles, self.stage = nc, core, tiles, stage
        sb, sem = stage.sbuf, stage.sem
        self.pre_st, self.post_st = sb("pre_stats", [128, 2, tiles, 6]), sb("post_stats", [128, 2, tiles, 6])
        self.pre_mv, self.post_mv = sb("pre_mean_var", [128, 2, tiles, 2]), sb("post_mean_var", [128, 2, tiles, 2])
        self.pre_rs, self.post_rs = sb("pre_rstd", [128, 2, tiles]), sb("post_rstd", [128, 2, tiles])
        self.xn = sb("x_normed", [128, 2, tiles, D])
        self.yn = sb("y_normed", [128, 2, tiles, D])
        self.pre_stats_done, self.pre_mv_done = sem("pre_stats_done"), sem("pre_mv_done")
        self.pre_eps_added, self.pre_rstd_done, self.xn_done = sem("pre_eps_added"), sem("pre_rstd_done"), sem("xn_done")
        self.post_stats_done, self.post_mv_done = sem("post_stats_done"), sem("post_mv_done")
        self.post_eps_added, self.post_rstd_done, self.yn_done = sem("post_eps_added"), sem("post_rstd_done"), sem("yn_done")
        self.yn_free = sem("yn_free")

    def tile(self, n, t):
        return self.core.x[:, bass.ds(self.tiles * n + t, 1), :]

    def pre_statistics(self, dve, n, s):
        if isinstance(n, int) and n < 2 and self.stage.first:
            dve.wait_ge(self.core.x_loaded, 16 * n + 16)
        for t in range(self.tiles):
            ins = dve.bn_stats(self.pre_st[:, s, t, :], self.tile(n, t))
        ins.then_inc(self.pre_stats_done, 1)
        wait_apart(dve, self.pre_stats_done, n + 1, self.core.dve_passed)
        for t in range(self.tiles):
            ins = dve.bn_aggr(self.pre_mv[:, s, t, :], self.pre_st[:, s, t, :])
        ins.then_inc(self.pre_mv_done, 1)

    def pre_rstd(self, pool, n, s):
        pool.wait_ge(self.pre_mv_done, n + 1)
        pool.tensor_tensor(self.pre_rs[:, s, :], self.pre_mv[:, s, :, 1], self.core.eps[:, 0:self.tiles], ALU.add)\
            .then_inc(self.pre_eps_added, 1)
        pool.wait_ge(self.pre_eps_added, n + 1)
        pool.tensor_tensor(self.pre_rs[:, s, :], self.pre_rs[:, s, :], self.core.half[:, 0:self.tiles], ALU.pow)\
            .then_inc(self.pre_rstd_done, 1)

    def pre_normalise(self, dve, n, s, transposed):
        dve.wait_ge(self.pre_rstd_done, n + 1)
        if transposed is not None:
            wait(dve, transposed, n - 1)
        for t in range(self.tiles):
            ins = dve.tensor_scalar(self.xn[:, s, t, :], self.tile(n, t), self.pre_mv[:, s, t, 0:1],
                                    self.pre_rs[:, s, t:t + 1], ALU.subtract, ALU.mult)
        ins.then_inc(self.xn_done, 1)

    def post_statistics(self, dve, n, s, y, arrived):
        if arrived is not None:
            dve.wait_ge(arrived, n + 1)
        for t in range(self.tiles):
            ins = dve.bn_stats(self.post_st[:, s, t, :], y[:, t, :])
        ins.then_inc(self.post_stats_done, 1)
        wait_apart(dve, self.post_stats_done, n + 1, self.core.dve_passed)
        for t in range(self.tiles):
            ins = dve.bn_aggr(self.post_mv[:, s, t, :], self.post_st[:, s, t, :])
        ins.then_inc(self.post_mv_done, 1)

    def post_rstd(self, pool, n, s):
        pool.wait_ge(self.post_mv_done, n + 1)
        pool.tensor_tensor(self.post_rs[:, s, :], self.post_mv[:, s, :, 1], self.core.eps[:, 0:self.tiles], ALU.add)\
            .then_inc(self.post_eps_added, 1)
        pool.wait_ge(self.post_eps_added, n + 1)
        pool.tensor_tensor(self.post_rs[:, s, :], self.post_rs[:, s, :], self.core.half[:, 0:self.tiles], ALU.pow)\
            .then_inc(self.post_rstd_done, 1)

    def post_normalise(self, dve, n, s, y):
        dve.wait_ge(self.post_rstd_done, n + 1)
        dve.wait_ge(self.yn_free, n + 1)
        for t in range(self.tiles):
            ins = dve.tensor_scalar(self.yn[:, s, t, :], y[:, t, :], self.post_mv[:, s, t, 0:1],
                                    self.post_rs[:, s, t:t + 1], ALU.subtract, ALU.mult)
        ins.then_inc(self.yn_done, 1)

    def store(self, sp):
        def block(n):
            wait_apart(sp, self.yn_free, n + 3, self.core.sp_passed)
            at = bass.ds(self.tiles * n, self.tiles)
            sp.dma_start(self.core.out[:, at, :], self.core.x[:, at, :]).then_inc(self.core.stored, 16)

        count = TILES // self.tiles
        blocks(sp, count, lambda n, s, first, last: block(n))
        sp.wait_ge(self.core.stored, 16 * count)

    def add_to_x(self, pool, n, s):
        pool.wait_ge(self.yn_done, n + 1)
        rows = self.core.x[:, bass.ds(self.tiles * n, self.tiles), :]
        pool.tensor_tensor(rows, rows, self.yn[:, s, :, :], ALU.add).then_inc(self.yn_free, 1)


class Item:

    def __init__(self, rows, func, buffer, gate=None, up=None, expert=None, bias=None, scale=None,
                 up_scale=None, deep=None):
        self.rows, self.func, self.buffer, self.gate, self.up, self.expert = rows, func, buffer, gate, up, expert
        self.bias, self.scale, self.up_scale, self.deep = bias, scale, up_scale, deep
        self.on_dve = up is not None or expert is not None


def ffn_stage(nc, core, name, items, down, at, weights, prepare=None, router=None, final_bias=None,
              final_scale=None):
    tiles, count, per = FFN_TILES, FFN_BLOCKS, len(items)
    buffers = max(i.buffer for i in items) + 1
    with ExitStack() as ctx:
        stage = Stage(nc, ctx, core, name)
        sb, sem, bank = stage.sbuf, stage.sem, stage.bank
        norms = Norms(nc, core, stage, tiles)
        xnT = sb("xnT", [128, 2, FFN_TOKENS])
        act = sb("activated", [128, 2, FFN_TOKENS])
        act_up = sb("activated_up", [128, 2, FFN_TOKENS])
        hid = sb("hidden", [128, buffers, FFN_TOKENS])
        yT = sb("yT", [128, FFN_TOKENS])
        G, U, C = ([bank(f"{b}{j}", [128, 512]) for j in range(2)] for b in "GUC")
        Y, T = bank("Y", [128, 512]), bank("T", [128, 512])
        T_tok = T[:, :].rearrange("p (t f) -> p t f", t=tiles)
        xn_transposed, xnT_done = sem("xn_transposed"), sem("xnT_done")
        item_full, activated = sem("item_full"), sem("activated")
        hidden_by_dve, hidden_by_act = sem("hidden_by_dve"), sem("hidden_by_act")
        up_applied = sem("up_applied")
        down_done, yT_done, y_transposed = sem("down_done"), sem("yT_done"), sem("y_transposed")
        weights_prepared = sem("weights_prepared")
        route = router(core, stage, T) if router else None

        first_expert = ([i.expert is not None for i in items] + [True]).index(True)
        on_dve = [i.on_dve for i in items]
        both = [k for k, i in enumerate(items) if i.up is not None and i.expert is not None]
        parity = lambda s, k: (s * per + k) % 2

        def wait_hidden(eng, n, k):
            if k < 0:
                n, k = n - 1, k + per
            if not (isinstance(n, int) and n < 0):
                mine = [x == on_dve[k] for x in on_dve]
                eng.wait_ge(hidden_by_dve if on_dve[k] else hidden_by_act, n * sum(mine) + sum(mine[:k + 1]))

        def last_use_of(k):
            found = [(down_done, len(down), j + 1) for j, (_, src) in enumerate(down) if src == k]
            found += [(item_full, per, j + 1) for j, i in enumerate(items) if i.deep and k in [q for _, q in i.deep]]
            return found[-1]

        def wait_buffer(eng, n, k):
            older = [q for q in range(k) if items[q].buffer == items[k].buffer]
            if older:
                s_, of, j = last_use_of(older[-1])
                eng.wait_ge(s_, n * of + j)
            elif not (isinstance(n, int) and n == 0):
                older = [q for q in range(per) if items[q].buffer == items[k].buffer]
                s_, of, j = last_use_of(older[-1])
                eng.wait_ge(s_, (n - 1) * of + j)

        with nc.Block() as block:
            @block.tensor
            def _(pe):
                def pre_transpose(n, s):
                    pe.wait_ge(norms.xn_done, n + 1)
                    wait(pe, norms.yn_done, n - 1)
                    for t in range(tiles):
                        ins = pe.transpose(T_tok[:, t, :], norms.xn[:, s, t, :], core.ident[:, :])
                    ins.then_inc(xn_transposed, 1)

                def post_transpose(n, s):
                    pe.wait_ge(yT_done, n + 1)
                    for t in range(tiles):
                        ins = pe.transpose(T_tok[:, t, :], yT[:, t * 128:t * 128 + 128], core.ident[:, :])
                    ins.then_inc(y_transposed, 1)

                def item(n, s, k):
                    it, b = items[k], parity(s, k)
                    wait_hidden(pe, n, k - 2)
                    if it.deep:
                        for j, (w, src) in enumerate(it.deep):
                            wait_hidden(pe, n, src)
                            ins = pe.matmul(G[b][0:it.rows, :], w, hid[:, items[src].buffer, :],
                                            start=j == 0, stop=j == len(it.deep) - 1)
                    else:
                        ins = pe.matmul(G[b][0:it.rows, :], it.gate, xnT[:, s, :], start=True, stop=True)
                    if it.up is not None:
                        ins = pe.matmul(U[b][0:it.rows, :], it.up, xnT[:, s, :], start=True, stop=True)
                    if it.expert is not None:
                        sel, half = it.expert
                        if k == first_expert:
                            pe.wait_ge(route.cwT_done, n + 1)
                        ins = pe.matmul(C[b][0:it.rows, :], sel, route.cwT[:, s, half, :], start=True, stop=True)
                    ins.then_inc(item_full, 1)

                def sum_up(n, s, j):
                    w, k = down[j]
                    wait_hidden(pe, n, k)
                    if j == 0:
                        wait(pe, yT_done, n)
                    more = route.extra_down if route else []
                    ins = pe.matmul(Y[:, :], w, hid[0:items[k].rows, items[k].buffer, :],
                                    start=j == 0, stop=j == len(down) - 1 and not more)
                    if j == len(down) - 1:
                        for q, (wx, half) in enumerate(more):
                            ins = pe.matmul(Y[:, :], wx, route.cwT[:, s, half, :], start=False,
                                            stop=q == len(more) - 1)
                    ins.then_inc(down_done, 1)

                def body(n, s, first, last):
                    pe.wait_ge(xnT_done, n + 1)
                    j = 0
                    for k in range(per):
                        item(n, s, k)
                        if route and first and k == first_expert - 1:
                            route.pe_transpose(pe, 0)
                            pe.wait_ge(route.cwT_done, 1)
                        if k == at["post"] and not first:
                            post_transpose(n - 1, 1 - s)
                        if k == at["pre"] and not last:
                            pre_transpose(n + 1, 1 - s)
                        if route and k == at["logits"] and not last:
                            route.pe_logits(pe, n + 1, xnT[:, 1 - s, :], xnT_done)
                        if route and k == at["experts"] and not last:
                            route.pe_transpose(pe, n + 1)
                        while j < len(down) and down[j][1] < k:
                            sum_up(n, s, j)
                            j += 1
                    while j < len(down):
                        sum_up(n, s, j)
                        j += 1

                for signal, c in weights:
                    pe.wait_ge(signal, c)
                if prepare:
                    pe.wait_ge(weights_prepared, 1)
                pre_transpose(0, 0)
                if route:
                    route.pe_logits(pe, 0, xnT[:, 0, :], xnT_done)
                    if first_expert == 0:
                        route.pe_transpose(pe, 0)
                blocks(pe, count, body)
                post_transpose(count - 1, (count - 1) % 2)

            @block.sync
            def _(sp):
                core.weights.prefetch(sp, name)
                if stage.last:
                    norms.store(sp)

            @block.scalar
            def _(eng):
                def copy_xnT(n, s):
                    eng.wait_ge(xn_transposed, n + 1)
                    wait(eng, item_full, (n - 1) * per)
                    eng.activation(xnT[:, s, :], T[:, :], ACT.Copy).then_inc(xnT_done, 1)

                def item(n, s, k):
                    it, b = items[k], parity(s, k)
                    eng.wait_ge(item_full, n * per + k + 1)
                    if it.on_dve:
                        wait_hidden(eng, n, k - 2)
                        out, done = act[0:it.rows, b, :], activated
                    else:
                        wait_buffer(eng, n, k)
                        out, done = hid[0:it.rows, it.buffer, :], hidden_by_act
                    eng.activation(out, G[b][0:it.rows, :], it.func,
                                   bias=core.zero[0:it.rows, :] if it.bias is None else it.bias,
                                   scale=1.0 if it.scale is None else it.scale).then_inc(done, 1)

                def copy_y(n, s):
                    eng.wait_ge(down_done, n * len(down) + len(down))
                    wait(eng, y_transposed, n)
                    eng.activation(yT[:, :], Y[:, :], ACT.Identity,
                                   bias=core.zero[:, :] if final_bias is None else final_bias,
                                   scale=1.0 if final_scale is None else final_scale).then_inc(yT_done, 1)

                def body(n, s, first, last):
                    for k in range(per):
                        item(n, s, k)
                        if route and first and k == first_expert - 1:
                            route.act_copy(eng, 0, 0, item_full, 0, down_done, 0)
                        if k == at["pre"] and not last:
                            copy_xnT(n + 1, 1 - s)
                        if route and k == at["exp"] and not last:
                            route.act_exp(eng, n + 1)
                        if route and k == at["experts"] and not last:
                            route.act_copy(eng, n + 1, 1 - s, item_full, (n + 1 - 1) * per, down_done, (n + 1 - 1) * len(down))
                    copy_y(n, s)

                for signal, c in weights:
                    eng.wait_ge(signal, c)
                if prepare:
                    eng.wait_ge(weights_prepared, 1)
                copy_xnT(0, 0)
                if route:
                    route.act_exp(eng, 0)
                    if first_expert == 0:
                        route.act_copy(eng, 0, 0, item_full, 0, down_done, 0)
                blocks(eng, count, body)

            @block.vector
            def _(dve):
                def item(n, s, k):
                    it, b = items[k], parity(s, k)
                    if not it.on_dve:
                        return
                    mine = sum(on_dve)
                    dve.wait_ge(activated, n * mine + sum(on_dve[:k + 1]))
                    wait_buffer(dve, n, k)
                    out, a = hid[0:it.rows, it.buffer, :], act[0:it.rows, b, :]
                    if it.up is not None:
                        if it.expert is not None:
                            wait_hidden(dve, n, k - 2)
                        to = act_up[0:it.rows, b, :] if it.expert is not None else out
                        if it.up_scale is not None:
                            ins = dve.scalar_tensor_tensor(to, U[b][0:it.rows, :], it.up_scale, a, ALU.mult, ALU.mult)
                        else:
                            ins = dve.tensor_tensor(to, U[b][0:it.rows, :], a, ALU.mult)
                        if it.expert is not None:
                            ins.then_inc(up_applied, 1)
                            dve.wait_ge(up_applied, n * len(both) + both.index(k) + 1)
                            a = act_up[0:it.rows, b, :]
                    if it.expert is not None:
                        ins = dve.tensor_tensor(out, C[b][0:it.rows, :], a, ALU.mult)
                    ins.then_inc(hidden_by_dve, 1)

                def body(n, s, first, last):
                    routing = route.dve_route(dve, n + 1) if route and not last else None
                    for k in range(per):
                        if k == at["statistics"] and not last:
                            norms.pre_statistics(dve, n + 1, 1 - s)
                        if k == at["normalise"] and not last:
                            norms.pre_normalise(dve, n + 1, 1 - s, xn_transposed)
                        item(n, s, k)
                        if k == at["post"] and not first:
                            norms.post_statistics(dve, n - 1, 1 - s, T_tok, y_transposed)
                            norms.post_normalise(dve, n - 1, 1 - s, T_tok)
                        for _ in range(at["pieces"] if routing and k >= at["route"] else 0):
                            next(routing, None)
                    for _ in routing or ():
                        pass

                for signal, c in weights:
                    dve.wait_ge(signal, c)
                if prepare:
                    prepare(dve, stage).then_inc(weights_prepared, 1)
                norms.pre_statistics(dve, 0, 0)
                norms.pre_normalise(dve, 0, 0, xn_transposed)
                if route:
                    route.dve_constants(dve)
                    for _ in route.dve_route(dve, 0):
                        pass
                blocks(dve, count, body)
                norms.post_statistics(dve, count - 1, (count - 1) % 2, T_tok, y_transposed)
                norms.post_normalise(dve, count - 1, (count - 1) % 2, T_tok)

            @block.gpsimd
            def _(pool):
                core.weights.prefetch_converted(pool, name)

                def body(n, s, first, last):
                    if not last:
                        norms.pre_rstd(pool, n + 1, 1 - s)
                    if not first:
                        norms.post_rstd(pool, n - 1, 1 - s)
                        norms.add_to_x(pool, n - 1, 1 - s)

                pool.sem_inc(norms.yn_free, 2)
                norms.pre_rstd(pool, 0, 0)
                blocks(pool, count, body)
                norms.post_rstd(pool, count - 1, (count - 1) % 2)
                norms.add_to_x(pool, count - 1, (count - 1) % 2)
        stage.clear()

class Router:

    def __init__(self, core, stage, T, weights, experts, halves, steps):
        self.nc, self.core, self.T, self.weights = core.nc, core, T, weights
        self.experts, self.halves, self.steps = experts, halves, steps
        t = FFN_TILES
        self.logits = T[:, 0:t * experts].rearrange("p (t e) -> p t e", t=t)
        self.parts = stage.sbuf("cw_parts", [128, t, halves, 3, experts // halves], BF16)
        self.cwT = stage.sbuf("cwT", [96 if 3 * experts // halves == 96 else 128, 2, halves, FFN_TOKENS], BF16)
        self.T16 = T[:, :].bitcast(BF16)
        self.cw, self.rest = stage.sbuf("cw", [128, t, experts]), stage.sbuf("cw_rest", [128, t, experts])
        self.e = stage.sbuf("router_exp", [128, t, experts])
        self.logits_full, self.exp_ready, self.exp_done = (
            stage.sem("logits_full"), stage.sem("exp_ready"), stage.sem("exp_done"))
        self.route_step, self.parts_transposed, self.cwT_done = (
            stage.sem("route_step"), stage.sem("parts_transposed"), stage.sem("cwT_done"))
        self.constants = stage.sem("router_constants")
        self.extra_down = []

    def pe_logits(self, pe, n, xnT, xnT_done):
        pe.wait_ge(xnT_done, n + 1)
        for t in range(FFN_TILES):
            ins = pe.matmul(self.logits[:, t, :], xnT[:, t * 128:t * 128 + 128], self.weights, start=True, stop=True)
        ins.then_inc(self.logits_full, 1)

    def pe_transpose(self, pe, n):
        wait_apart(pe, self.route_step, n * self.steps + self.steps, self.core.pe_passed)
        rows = 3 * self.experts // self.halves
        for h in range(self.halves):
            for t in range(FFN_TILES):
                at = h * FFN_TOKENS + t * 128
                ins = pe.transpose(self.T16[0:rows, at:at + 128],
                                   self.parts[:, t, h, :, :].rearrange("p q e -> p (q e)"), self.core.ident16[:, :])
        ins.then_inc(self.parts_transposed, 1)

    def act_copy(self, eng, n, s, item_full, items_before, down_done, down_before):
        eng.wait_ge(self.parts_transposed, n + 1)
        if isinstance(n, int) and n == 0:
            eng.wait_ge(self.constants, 1)
        wait(eng, item_full, items_before)
        wait(eng, down_done, down_before)
        rows = 3 * self.experts // self.halves
        eng.activation(self.cwT[0:rows, s, :, :],
                       self.T16[0:rows, 0:self.halves * FFN_TOKENS].rearrange("p (h n) -> p h n", h=self.halves),
                       ACT.Copy).then_inc(self.cwT_done, 1)

    def split(self, c):
        dve = c.eng
        view = lambda a: a[:, :, :].rearrange("p t (h e) -> p t h e", h=self.halves)
        part = lambda q: self.parts[:, :, :, q, :]
        c.link(dve.tensor_copy(part(0), view(self.cw)))
        c.link(dve.tensor_tensor(view(self.rest), view(self.cw), part(0), ALU.subtract))
        yield
        c.link(dve.tensor_copy(part(1), view(self.rest)))
        c.link(dve.tensor_tensor(view(self.rest), view(self.rest), part(1), ALU.subtract))
        c.last(dve.tensor_copy(part(2), view(self.rest)))


class SoftmaxRouter(Router):
    EXPERTS, TOP, STEPS = 64, 8, 17

    def __init__(self, core, stage, T, weights, bias):
        super().__init__(core, stage, T, weights, self.EXPERTS, 2, self.STEPS)
        self.bias = bias
        t = FFN_TILES
        self.lg = stage.sbuf("logits", [128, t, self.EXPERTS])
        self.col = stage.sbuf("router_columns", [128, 5, t])
        self.top, self.left = stage.sbuf("top8", [128, t, 8]), stage.sbuf("left", [128, t, self.EXPERTS])

    def act_exp(self, eng, n):
        eng.wait_ge(self.exp_ready, n + 1)
        eng.activation(self.e[:, :, :], self.lg[:, :, :], ACT.Exp, bias=self.core.zero[:, :]).then_inc(self.exp_done, 1)

    def dve_constants(self, dve):
        dve.memset(self.cwT[:, :, :, :], 0.0).then_inc(self.constants, 1)

    def dve_route(self, dve, n):
        E, t = self.EXPERTS, FFN_TILES
        wide = lambda q: self.col[:, q, :].rearrange("p (t o) -> p t o", o=1).to_broadcast([128, t, E])
        bias = self.bias.rearrange("p (o e) -> p o e", o=1).to_broadcast([128, t, E])
        c = Chain(dve, self.route_step, n, self.STEPS)
        dve.wait_ge(self.logits_full, n + 1)
        c.link(dve.tensor_tensor(self.lg[:, :, :], self.logits, bias, ALU.add))
        c.link(dve.tensor_reduce(self.col[:, 0, :], self.lg[:, :, :], AX.X, ALU.max))
        dve.tensor_tensor(self.lg[:, :, :], self.lg[:, :, :], wide(0), ALU.subtract).then_inc(self.exp_ready, 1)
        yield
        dve.wait_ge(self.exp_done, n + 1)
        c.link(dve.tensor_reduce(self.col[:, 1, :], self.e[:, :, :], AX.X, ALU.add))
        c.link(dve.reciprocal(self.col[:, 2, :], self.col[:, 1, :]))
        c.link(dve.tensor_tensor(self.e[:, :, :], self.e[:, :, :], wide(2), ALU.mult), self.core.dve_passed)
        yield
        for q in range(t):
            ins = dve.max(self.top[:, q, :], self.e[:, q, :])
        c.link(ins, self.core.dve_passed)
        for q in range(t):
            ins = dve.match_replace(self.left[:, q, :], self.top[:, q, :], self.e[:, q, :], -1.0)
        c.link(ins)
        yield
        c.link(dve.tensor_reduce(self.col[:, 3, :], self.top[:, :, :], AX.X, ALU.add))
        c.link(dve.reciprocal(self.col[:, 4, :], self.col[:, 3, :]))
        c.link(dve.tensor_scalar(self.left[:, :, :], self.left[:, :, :], 0.0, None, ALU.is_lt))
        yield
        c.link(dve.tensor_tensor(self.left[:, :, :], self.left[:, :, :], self.e[:, :, :], ALU.mult))
        c.link(dve.tensor_tensor(self.cw[:, :, :], self.left[:, :, :], wide(4), ALU.mult))
        yield
        yield from self.split(c)


class GroupRouter(Router):
    EXPERTS, GROUPS, TOP_GROUPS, TOP, SCALE, STEPS = 16, 4, 2, 4, 2.5, 29
    NEVER, TAKEN = 3.0e38, 3.2e38

    def __init__(self, core, stage, T, weights, bias):
        super().__init__(core, stage, T, weights, self.EXPERTS, 1, self.STEPS)
        self.bias = bias
        t, E, g = FFN_TILES, self.EXPERTS, self.GROUPS
        self.s, self.sb = stage.sbuf("scores", [128, t, E]), stage.sbuf("biased", [128, t, E])
        self.pairs, self.best = stage.sbuf("pairs", [128, t * g, 6]), stage.sbuf("group_best", [128, t, 8])
        self.top, self.seek = stage.sbuf("top8", [128, t, 8]), stage.sbuf("seek", [128, t, 8])
        self.seek_e, self.left = stage.sbuf("seek_experts", [128, t, 8]), stage.sbuf("groups_left", [128, t, 8])
        self.mask, self.off = stage.sbuf("group_mask", [128, t * g]), stage.sbuf("group_off", [128, t * g])
        self.m, self.mr = stage.sbuf("masked", [128, t, E]), stage.sbuf("masked_left", [128, t, E])
        self.col = stage.sbuf("router_columns", [128, 4, t])

    def act_exp(self, eng, n):
        eng.wait_ge(self.logits_full, n + 1)
        eng.activation(self.e[:, :, :], self.logits, ACT.Exp, bias=self.core.zero[:, :], scale=-1.0)\
            .then_inc(self.exp_done, 1)

    def dve_constants(self, dve):
        dve.memset(self.best[:, :, :], -self.NEVER)
        dve.memset(self.seek[:, :, :], self.NEVER)
        dve.memset(self.seek_e[:, :, :], self.NEVER)
        dve.memset(self.cwT[:, :, :, :], 0.0).then_inc(self.constants, 1)
        dve.wait_ge(self.constants, 1)

    def dve_route(self, dve, n):
        E, G, t, k = self.EXPERTS, self.GROUPS, FFN_TILES, self.EXPERTS // self.GROUPS
        by_group = lambda a: a[:, :, :].rearrange("p t (g k) -> p (t g) k", g=G)
        over = lambda a: a[:, :].rearrange("p (q o) -> p q o", o=1).to_broadcast([128, t * G, k])
        c = Chain(dve, self.route_step, n, self.STEPS)
        bias = self.bias.rearrange("p (o e) -> p o e", o=1).to_broadcast([128, t, E])
        dve.wait_ge(self.exp_done, n + 1)
        c.link(dve.tensor_scalar(self.s[:, :, :], self.e[:, :, :], 1.0, None, ALU.add))
        c.link(dve.reciprocal(self.s[:, :, :], self.s[:, :, :]))
        c.link(dve.tensor_tensor(self.sb[:, :, :], self.s[:, :, :], bias, ALU.add))
        yield
        v = by_group(self.sb)
        c.link(dve.tensor_tensor(self.pairs[:, :, 0:3], v[:, :, 0:3], v[:, :, 1:4], ALU.add))
        c.link(dve.tensor_tensor(self.pairs[:, :, 3:5], v[:, :, 0:2], v[:, :, 2:4], ALU.add))
        c.link(dve.tensor_tensor(self.pairs[:, :, 5:6], v[:, :, 0:1], v[:, :, 3:4], ALU.add))
        yield
        c.link(dve.tensor_reduce(self.best[:, :, 0:G], self.pairs[:, :, :].rearrange("p (t g) k -> p t g k", t=t),
                                 AX.X, ALU.max), self.core.dve_passed)
        for q in range(t):
            ins = dve.max(self.top[:, q, :], self.best[:, q, :])
        c.link(ins)
        yield
        c.link(dve.tensor_copy(self.seek[:, :, 0:self.TOP_GROUPS], self.top[:, :, 0:self.TOP_GROUPS]), self.core.dve_passed)
        for q in range(t):
            ins = dve.match_replace(self.left[:, q, :], self.seek[:, q, :], self.best[:, q, :], self.TAKEN)
        c.link(ins)
        yield
        c.link(dve.tensor_scalar(self.mask[:, :].rearrange("p (t g) -> p t g", t=t), self.left[:, :, 0:G],
                                 self.NEVER * 1.03, None, ALU.is_gt))
        c.link(dve.tensor_scalar(self.off[:, :], self.mask[:, :], -1.0, 1.0e30, ALU.add, ALU.mult))
        yield
        c.link(dve.tensor_tensor(by_group(self.m), v, over(self.mask), ALU.mult))
        c.link(dve.tensor_tensor(by_group(self.m), by_group(self.m), over(self.off), ALU.add), self.core.dve_passed)
        for q in range(t):
            ins = dve.max(self.top[:, q, :], self.m[:, q, :])
        c.link(ins)
        yield
        c.link(dve.tensor_copy(self.seek_e[:, :, 0:self.TOP], self.top[:, :, 0:self.TOP]), self.core.dve_passed)
        for q in range(t):
            ins = dve.match_replace(self.mr[:, q, :], self.seek_e[:, q, :], self.m[:, q, :], self.TAKEN)
        c.link(ins)
        yield
        c.link(dve.tensor_scalar(self.mr[:, :, :], self.mr[:, :, :], self.NEVER * 1.03, None, ALU.is_gt))
        c.link(dve.tensor_tensor(self.m[:, :, :], self.mr[:, :, :], self.s[:, :, :], ALU.mult))
        c.link(dve.tensor_reduce(self.col[:, 0, :], self.m[:, :, :], AX.X, ALU.add))
        yield
        c.link(dve.tensor_scalar(self.col[:, 1, :], self.col[:, 0, :], 1e-20, None, ALU.add))
        c.link(dve.reciprocal(self.col[:, 2, :], self.col[:, 1, :]))
        c.link(dve.tensor_scalar(self.col[:, 3, :], self.col[:, 2, :], self.SCALE, None, ALU.mult))
        yield
        total = self.col[:, 3, :].rearrange("p (t o) -> p t o", o=1).to_broadcast([128, t, E])
        c.link(dve.tensor_tensor(self.cw[:, :, :], self.m[:, :, :], total, ALU.mult))
        yield
        yield from self.split(c)

def attention0(nc, core):
    w, name, tiles, count = core.w, "L0a", FFN_TILES, FFN_BLOCKS
    SCALE = float(np.float32(1.0) / np.sqrt(np.float32(D)))
    with ExitStack() as ctx:
        stage = Stage(nc, ctx, core, name)
        sb, sem, bank = stage.sbuf, stage.sem, stage.bank
        norms = Norms(nc, core, stage, tiles)
        xnT, qT, kT = sb("xnT", [128, 2, 512]), sb("qT", [128, 2, 512]), sb("kT", [128, 2, 512])
        v = sb("v", [128, 2, tiles, D])
        scores, prob = sb("scores", [128, 2, 2, SEQ]), sb("prob", [128, 2, 2, SEQ])
        nmax, total, inv = sb("neg_max", [128, 2, 2]), sb("total", [128, 2, 2]), sb("inv_total", [128, 2, 2])
        probT, oT, y = sb("probT", [128, 2, 2, SEQ]), sb("oT", [128, 2, SEQ]), sb("y", [128, tiles, D])
        T, A, B, V, O, Y = (bank(b, [128, 512]) for b in ("T", "A", "B", "V", "O", "Y"))
        S = [bank(f"S{b}", [128, 512]) for b in range(2)]
        by_tile = lambda a: a[:, :].rearrange("p (t f) -> p t f", t=tiles)
        by_half = lambda a: a[:, :].rearrange("p (h f) -> p h f", h=2)
        xn_transposed, xnT_done = sem("xn_transposed"), sem("xnT_done")
        proj_full, q_done, k_done, v_done = sem("proj_full"), sem("q_done"), sem("k_done"), sem("v_done")
        s_full, soft_step, max_done, exp_done = sem("s_full"), sem("soft_step"), sem("max_done"), sem("exp_done")
        inv_done, p_done, pt_full, pT_done = sem("inv_done"), sem("p_done"), sem("pt_full"), sem("pT_done")
        o_full, oT_done, y_full, y_biased = sem("o_full"), sem("oT_done"), sem("y_full"), sem("y_biased")

        with nc.Block() as block:
            @block.tensor
            def _(pe):
                def pre_transpose(n, s):
                    pe.wait_ge(norms.xn_done, n + 1)
                    wait(pe, xnT_done, n)
                    for t in range(tiles):
                        ins = pe.transpose(by_tile(T)[:, t, :], norms.xn[:, s, t, :], core.ident[:, :])
                    ins.then_inc(xn_transposed, 1)

                def project(n, s):
                    pe.wait_ge(xnT_done, n + 1)
                    wait(pe, q_done, n)
                    pe.matmul(A[:, :], w["L0a_wq"][:, :], xnT[:, s, :], start=True, stop=True).then_inc(proj_full, 1)
                    wait(pe, k_done, n)
                    pe.matmul(B[:, :], w["L0a_wk"][:, :], xnT[:, s, :], start=True, stop=True).then_inc(proj_full, 1)
                    wait(pe, v_done, n)
                    for t in range(tiles):
                        ins = pe.matmul(by_tile(V)[:, t, :], xnT[:, s, t * 128:t * 128 + 128], w["L0a_wv"][:, :],
                                        start=True, stop=True)
                    ins.then_inc(proj_full, 1)

                def result(n):
                    pe.wait_ge(oT_done, n + 1)
                    wait(pe, y_biased, n)
                    for t in range(tiles):
                        ins = pe.matmul(by_tile(Y)[:, t, :], oT[:, t // 2, (t % 2) * 128:(t % 2) * 128 + 128],
                                        w["L0a_wo"][:, :], start=True, stop=True)
                    ins.then_inc(y_full, 1)

                def body(n, s, first, last):
                    pe.wait_ge(q_done, n + 1)
                    pe.wait_ge(k_done, n + 1)
                    for b in range(2):
                        if not first:
                            pe.wait_ge(pT_done, 2 * n + b - 1)
                        for h in range(2):
                            at = b * SEQ + h * 128
                            ins = pe.matmul(by_half(S[b])[:, h, :], qT[:, s, at:at + 128],
                                            kT[:, s, b * SEQ:b * SEQ + SEQ], start=True, stop=True)
                        ins.then_inc(s_full, 1)
                    if not first:
                        result(n - 1)
                    if not last:
                        pre_transpose(n + 1, 1 - s)
                        project(n + 1, 1 - s)
                    pe.wait_ge(v_done, n + 1)
                    for b in range(2):
                        pe.wait_ge(p_done, 2 * n + b + 1)
                        for k in range(2):
                            for h in range(2):
                                ins = pe.transpose(S[b][:, k * SEQ + h * 128:k * SEQ + h * 128 + 128],
                                                   prob[:, b, h, k * 128:k * 128 + 128], core.ident[:, :])
                        ins.then_inc(pt_full, 1)
                    for b in range(2):
                        pe.wait_ge(pT_done, 2 * n + b + 1)
                        if b == 0:
                            wait(pe, oT_done, n)
                        for k in range(2):
                            ins = pe.matmul(by_half(O)[:, b, :], v[:, s, 2 * b + k, :], probT[:, b, k, :],
                                            start=k == 0, stop=k == 1)
                        ins.then_inc(o_full, 1)

                pre_transpose(0, 0)
                for signal, c in core.loaded(name):
                    pe.wait_ge(signal, c)
                project(0, 0)
                blocks(pe, count, body)
                result(count - 1)

            @block.sync
            def _(sp):
                core.weights.prefetch(sp, name)
                if stage.last:
                    norms.store(sp)

            @block.scalar
            def _(eng):
                def copy_xnT(n, s):
                    eng.wait_ge(xn_transposed, n + 1)
                    wait(eng, proj_full, 3 * n - 3)
                    eng.activation(xnT[:, s, :], T[:, :], ACT.Copy).then_inc(xnT_done, 1)

                def qk(n, s):
                    wait(eng, s_full, 2 * n - 2)
                    eng.wait_ge(proj_full, 3 * n + 1)
                    eng.activation(qT[:, s, :], A[:, :], ACT.Identity, bias=w["L0a_bq"][:, :]).then_inc(q_done, 1)
                    eng.wait_ge(proj_full, 3 * n + 2)
                    eng.activation(kT[:, s, :], B[:, :], ACT.Identity, bias=w["L0a_bk"][:, :]).then_inc(k_done, 1)

                def exps(n, b):
                    eng.wait_ge(max_done, 2 * n + b + 1)
                    for h in range(2):
                        ins = eng.activation(prob[:, b, h, :], scores[:, b, h, :], ACT.Exp, bias=nmax[:, b, h:h + 1],
                                             accum_out=total[:, b, h:h + 1])
                    ins.then_inc(exp_done, 1)

                def body(n, s, first, last):
                    if not last:
                        copy_xnT(n + 1, 1 - s)
                    exps(n, 0)
                    exps(n, 1)
                    if not last:
                        qk(n + 1, 1 - s)
                    for b in range(2):
                        eng.wait_ge(pt_full, 2 * n + b + 1)
                        if not first:
                            eng.wait_ge(o_full, 2 * n + b - 1)
                        eng.activation(probT[:, b, :, :], by_half(S[b]), ACT.Copy).then_inc(pT_done, 1)
                    eng.wait_ge(o_full, 2 * n + 2)
                    wait(eng, y_full, n)
                    eng.activation(oT[:, :, :], by_half(O), ACT.Copy).then_inc(oT_done, 1)

                copy_xnT(0, 0)
                for signal, c in core.loaded(name):
                    eng.wait_ge(signal, c)
                qk(0, 0)
                blocks(eng, count, body)

            @block.vector
            def _(dve):
                def copy_v(n, s):
                    dve.wait_ge(proj_full, 3 * n + 3)
                    wait(dve, o_full, 2 * n - 2)
                    bias = w["L0a_bv"][:, :].rearrange("p (o f) -> p o f", o=1).to_broadcast([128, tiles, D])
                    dve.tensor_tensor(v[:, s, :, :], by_tile(V), bias, ALU.add).then_inc(v_done, 1)

                def scores_of(n, b):
                    dve.wait_ge(s_full, 2 * n + b + 1)
                    c = Chain(dve, soft_step, n, 4)
                    c.j = 2 * b
                    c.link(dve.scalar_tensor_tensor(scores[:, b, :, :], by_half(S[b]), SCALE, w["L0a_keep"][:, :, :],
                                                    ALU.mult, ALU.mult))
                    c.link(dve.tensor_tensor(scores[:, b, :, :], scores[:, b, :, :], w["L0a_never"][:, :, :], ALU.add))
                    dve.tensor_reduce(nmax[:, b, :], scores[:, b, :, :], AX.X, ALU.max, negate=True)\
                        .then_inc(max_done, 1)

                def probabilities(n, b):
                    dve.wait_ge(exp_done, 2 * n + b + 1)
                    dve.reciprocal(inv[:, b, :], total[:, b, :]).then_inc(inv_done, 1)
                    dve.wait_ge(inv_done, 2 * n + b + 1)
                    for h in range(2):
                        ins = dve.tensor_scalar(prob[:, b, h, :], prob[:, b, h, :], inv[:, b, h:h + 1], None, ALU.mult)
                    ins.then_inc(p_done, 1)

                def add_bias(n, s):
                    dve.wait_ge(y_full, n + 1)
                    wait(dve, norms.yn_done, n)
                    bias = w["L0a_bo"][:, :].rearrange("p (o f) -> p o f", o=1).to_broadcast([128, tiles, D])
                    dve.tensor_tensor(y[:, :, :], by_tile(Y), bias, ALU.add).then_inc(y_biased, 1)

                def body(n, s, first, last):
                    scores_of(n, 0)
                    scores_of(n, 1)
                    if not first:
                        add_bias(n - 1, 1 - s)
                    probabilities(n, 0)
                    probabilities(n, 1)
                    if not first:
                        norms.post_statistics(dve, n - 1, 1 - s, y, y_biased)
                    if not last:
                        copy_v(n + 1, 1 - s)
                        norms.pre_statistics(dve, n + 2, s)
                    if not first:
                        norms.post_normalise(dve, n - 1, 1 - s, y)
                    if not last:
                        norms.pre_normalise(dve, n + 2, s, xn_transposed)

                for n in range(2):
                    norms.pre_statistics(dve, n, n)
                    norms.pre_normalise(dve, n, n, xn_transposed)
                for signal, c in core.loaded(name):
                    dve.wait_ge(signal, c)
                copy_v(0, 0)
                blocks(dve, count, body)
                add_bias(count - 1, (count - 1) % 2)
                norms.post_statistics(dve, count - 1, (count - 1) % 2, y, y_biased)
                norms.post_normalise(dve, count - 1, (count - 1) % 2, y)

            @block.gpsimd
            def _(pool):
                core.weights.prefetch_converted(pool, name)

                def body(n, s, first, last):
                    if not first:
                        norms.post_rstd(pool, n - 1, 1 - s)
                    if not last:
                        norms.pre_rstd(pool, n + 2, s)
                    if not first:
                        norms.add_to_x(pool, n - 1, 1 - s)

                pool.sem_inc(norms.yn_free, 2)
                norms.pre_rstd(pool, 0, 0)
                norms.pre_rstd(pool, 1, 1)
                blocks(pool, count, body)
                norms.post_rstd(pool, count - 1, (count - 1) % 2)
                norms.add_to_x(pool, count - 1, (count - 1) % 2)
        stage.clear()

class Turns:

    def __init__(self, stage, name, slots, uses):
        self.keys, self.engines, self.slots = [u[0] for u in uses], [u[1] for u in uses], slots
        assert len(uses) % slots == 0
        self.filled = stage.sem(f"{name}_filled")
        self.by = {e: stage.sem(f"{name}_emptied_by_{e}") for e in sorted(set(self.engines))}

    def slot(self, key):
        return self.keys.index(key) % self.slots

    def filling(self, k, key):
        return self.filled, k * len(self.keys) + self.keys.index(key) + 1

    def emptying(self, k, key, back=0):
        i = self.keys.index(key) - back
        k, i = (k, i) if i >= 0 else (k - 1, i + len(self.keys))
        e = self.engines[i]
        return self.by[e], k * self.engines.count(e) + self.engines[:i + 1].count(e)

    def last(self, k, key):
        return self.emptying(k, key, self.slots)

    def emptied(self, key):
        return self.by[self.engines[self.keys.index(key)]]

    def skip_filling(self, pe, k, key):
        wait(pe, *self.last(k, key))
        sem, count = self.filling(k, key)
        wait(pe, sem, count - 1)
        pe.sem_inc(sem, 1)

    def skip_emptying(self, eng, k, key):
        sem, count = self.emptying(k, key)
        wait(eng, sem, count - 1)
        eng.sem_inc(sem, 1)


def rope_attention(nc, core, name):
    w, tiles, count, HALF = core.w, FFN_TILES, FFN_BLOCKS, HEADS // 2
    SCALE = 1.0 / float(np.sqrt(np.float32(HD)))
    W = lambda k: w[f"{name}_{k}"]
    ROWS = 9 * HD

    LOADS = 7 * 16

    def steps():
        for p in range(2):
            cur, nxt = p, 1 - p
            at0, at1 = (lambda *s: [s] if p == 0 else []), (lambda *s: [s] if p == 1 else [])
            yield from [("score", nxt, 0), *at0("stats"), ("exp", cur, 0), ("score", nxt, 2), ("maxT", cur, 1),
                        ("pv", nxt, 3), ("exp", cur, 1), ("score", nxt, 1), ("exp", cur, 2), *at0("norm"),
                        ("oT", nxt, 1), ("score", nxt, 3), ("exp", cur, 3), *at1("part", 1), ("score", nxt, 4),
                        *at0("xT"), ("pv", cur, 0), ("split", nxt, 0), ("exp", cur, 4), ("score", nxt, 5),
                        ("attT", nxt), *at0("q"), *at1("part", 2), *at0("y"), ("pv", cur, 1), ("maxT", nxt, 0),
                        *at0("k"), ("score", nxt, 6), ("exp", cur, 5), ("oT", cur, 0), *at0("v"),
                        ("score", nxt, 7), ("split", nxt, 1), ("exp", cur, 6), *at1("store"), *at0("post"),
                        *at0("part", 0), ("exp", cur, 7), ("pv", cur, 2),
                        *at0("half done")]

    STEPS = list(steps())

    def absent(n, i):
        if not isinstance(n, int):
            return False
        step = STEPS[i]
        kind = step[0]
        p = int(i > STEPS.index(("half done",)))
        if kind in ("score", "split"):
            m = n if p == 0 else n + 1
            return m < 0 or m >= count
        if kind == "maxT":
            m = n + 1 if p == 1 and step[1] == 0 else n
            return m < 0 or m >= count
        if kind == "exp":
            return n < 0
        if kind in ("pv", "oT", "attT"):
            m = n - 1 if p == 0 and step[1] == 1 else n
            return m < 0
        if kind in ("y", "post"):
            return n - 1 < 0
        if kind == "v":
            return not 0 <= n + 1 < count
        return n + 2 >= count

    with ExitStack() as ctx:
        stage = Stage(nc, ctx, core, name)
        sb, sem, bank = stage.sbuf, stage.sem, stage.bank
        norms = Norms(nc, core, stage, tiles)
        xnT = sb("xnT", [128, 2, 512])
        rot, qk = sb("rotated", [128, 2, 2, 512]), sb("qk", [128, 2, 512])
        parts = sb("parts", [128, 2, 3, 512], BF16)
        stack = [[sb(f"{x}_stack{b}", [96, HEADS, SEQ], BF16) for x in "qk"] for b in range(2)]
        V32 = sb("v", [128, 2, tiles, HEADS, 32])
        nmax, rest = sb("neg_max", [128, 2, 2, 2, HALF]), sb("max_rest", [128, 2, HALF])
        mparts, M = sb("max_parts", [128, 2, 2, 2, 3, HALF], BF16), sb("maxT", [3 * HALF, 2, 2, SEQ], BF16)
        fixed = sb("fixed_rows", [3, 2, HALF, SEQ], BF16)
        P = sb("expT", [128, 4, 2, 2, SEQ])
        O_sb, att, attT = sb("oT", [128, 2, 2, SEQ]), sb("att", [128, 2, 2, D]), sb("attT", [128, 2, SEQ])
        rsum, y = sb("inv_sum", [128, 4, 4]), sb("y", [128, tiles, D])
        chunk = [bank(f"R{i}", [128, 1024]) for i in range(3)]
        T, O = bank("T", [128, 512]), bank("O", [128, 2, SEQ])
        T16 = T[:, :].bitcast(BF16)
        scratch = nc.dram_tensor(f"{name}_scratch", (2, 2, 6, 128, SEQ), BF16).ap()

        ring_of = {"score": "dve", "exp": "act", "q": "dve", "k": "dve", "v": "dve", "y": "dve"}
        R = Turns(stage, "chunk", 3, [(s, ring_of[s[0]]) for s in STEPS if s[0] in ring_of])
        t_of = {"xT": "act", "maxT": "act", "oT": "dve", "attT": "act"}
        TR = Turns(stage, "T", 1, [(s, t_of[s[0]]) for s in STEPS if s[0] in t_of])
        OR = Turns(stage, "O", 1, [(s, "act") for s in STEPS if s[0] == "pv" and s[2] % 2 == 1])
        pv_done, split_step, rope_done, added = sem("pv_done"), sem("split_step"), sem("rope_done"), sem("added")
        part_done, rest_done = sem("part_done"), sem("rest_done")
        stored = [sem(f"parts_of_{b}_stored") for b in range(2)]
        loaded = [[sem(f"stack{b}{h}_loaded") for h in range(2)] for b in range(2)]
        sums_done, v_cleared, cleared = sem("sums_done"), sem("v_cleared"), sem("cleared")
        stack_cleared, pool_cleared, ones_loaded = sem("stack_cleared"), sem("pool_cleared"), sem("ones_loaded")
        max_loaded = [[sem(f"max{b}{h}_loaded") for h in range(2)] for b in range(2)]
        splits = [s for s in STEPS if s[0] == "split"]
        pvs = [s for s in STEPS if s[0] == "pv" and s[2] % 2 == 0]
        oTs = [s for s in STEPS if s[0] == "oT"]

        def k_of(n):
            return n + 2

        def wait_pv(eng, k, step):
            if step[2] % 2:
                wait(eng, *OR.filling(k, step))
            else:
                eng.wait_ge(pv_done, k * 4 + pvs.index(step) + 1)

        def block_of(n, i):
            p = int(i > STEPS.index(("half done",)))
            kind = STEPS[i][0]
            if kind in ("score", "split"):
                return n if p == 0 else n + 1
            if kind == "maxT":
                return n + 1 if p == 1 and STEPS[i][1] == 0 else n
            return n - 1 if p == 0 and STEPS[i][1] == 1 and kind != "exp" else n

        def bodies(eng, body):
            for n in (-2, -1, 0):
                body(n, n % 2)
            with eng.Fori(0, (count - 2) // 2) as i:
                body(2 * i + 1, 1)
                body(2 * i + 2, 0)
            body(count - 1, (count - 1) % 2)
            body(count, count % 2)

        def present(n, i):
            if isinstance(n, int) and n == count:
                p0 = i < STEPS.index(("half done",))
                return p0 and (STEPS[i][0] in ("y", "post") or STEPS[i] in (("pv", 1, 3), ("oT", 1, 1), ("attT", 1)))
            return not absent(n, i)

        with nc.Block() as block:
            @block.tensor
            def _(pe):
                def body(n, s):
                    k = k_of(n)
                    if isinstance(n, int) and n == -1:
                        pe.wait_ge(ones_loaded, 4 * 16)
                    for i, step in enumerate(STEPS):
                        kind, b = step[0], step[1] if len(step) > 1 else None
                        ring = R if kind in ring_of else TR if kind in t_of else None
                        if not present(n, i):
                            if ring:
                                ring.skip_filling(pe, k, step)
                            if kind == "pv" and step[2] % 2:
                                OR.skip_filling(pe, k, step)
                            elif kind == "pv":
                                wait(pe, pv_done, k * 4 + pvs.index(step))
                                pe.sem_inc(pv_done, 1)
                            continue
                        if kind == "score":
                            c = step[2]
                            m = block_of(n, i)
                            if c % 4 == 0:
                                pe.wait_ge(loaded[b][c // 4], LOADS * m + LOADS)
                            wait(pe, *R.last(k, step))
                            out = chunk[R.slot(step)][:, :].rearrange("p (h t) -> p h t", h=4)
                            for q in range(4):
                                h, at = 4 * (c // 2) + q, (c % 2) * 128
                                ins = pe.matmul(out[:, q, :], stack[b][0][:, h, at:at + 128], stack[b][1][:, h, :],
                                                start=True, stop=True)
                            ins.then_inc(R.filled, 1)
                        elif kind == "exp":
                            j = step[2]
                            if j % 4 == 0:
                                pe.wait_ge(max_loaded[b][j // 4], 16 * n + 16)
                            wait(pe, *R.last(k, step))
                            out = chunk[R.slot(step)][:, :].rearrange("p (h k t) -> p h k t", h=2, k=2)
                            for q in range(2):
                                h = 2 * j + q
                                for kt in range(2):
                                    ins = pe.matmul(out[:, q, kt, :], stack[b][1][:, h, kt * 128:kt * 128 + 128],
                                                    stack[b][0][:, h, :], start=True, stop=True)
                            ins.then_inc(R.filled, 1)
                        elif kind == "pv":
                            g = step[2]
                            sv = s if block_is_this(i) else 1 - s
                            kk = k if block_is_this(i) else k - 1
                            wait(pe, *R.emptying(kk, ("exp", b, 2 * g + 1)))
                            if g % 2 == 0:
                                wait(pe, *OR.last(k + 1 if (b, g) == (1, 2) else k, ("pv", b, g + 1)))
                                wait(pe, *R.emptying(kk - 1, ("v",)))
                            for kt in range(2):
                                for q in range(4):
                                    c = 2 * g + q // 2
                                    ins = pe.matmul(O[32 * q:32 * q + 32, g % 2, :], V32[:, sv, 2 * b + kt, 4 * g + q, :],
                                                    P[:, c % 4, q % 2, kt, :], start=kt == 0, stop=kt == 1,
                                                    tile_position=(0, 32 * q))
                            ins.then_inc(OR.filled if g % 2 else pv_done, 1)
                        elif kind == "oT":
                            h = step[2]
                            wait(pe, *OR.emptying(k, ("pv", b, 2 * h + 1)))
                            wait(pe, *TR.last(k, step))
                            for qt in range(2):
                                for g in range(2):
                                    at = (2 * qt + g) * 128
                                    ins = pe.transpose(T[:, at:at + 128], O_sb[:, h, g, qt * 128:qt * 128 + 128],
                                                       core.ident[:, :])
                            ins.then_inc(TR.filled, 1)
                        elif kind == "attT":
                            wait(pe, *TR.emptying(k, ("oT", b, 1)))
                            wait(pe, *TR.last(k, step))
                            for qt in range(2):
                                ins = pe.transpose(T[:, qt * 128:qt * 128 + 128], att[:, b, qt, :], core.ident[:, :])
                            ins.then_inc(TR.filled, 1)
                        elif kind == "maxT":
                            h = step[2]
                            kk = k - 1 if b == 0 and h == 1 else k
                            pe.wait_ge(split_step, kk * 20 + 5 * splits.index(("split", b, h)) + 5)
                            wait(pe, *TR.last(k, step))
                            for qt in range(2):
                                ins = pe.transpose(T16[0:3 * HALF, qt * 128:qt * 128 + 128],
                                                   mparts[:, b, h, qt, :, :].rearrange("p q e -> p (q e)"),
                                                   core.ident16[:, :])
                            ins.then_inc(TR.filled, 1)
                        elif kind == "xT":
                            pe.wait_ge(norms.xn_done, n + 3)
                            wait(pe, *TR.last(k, step))
                            for t in range(tiles):
                                ins = pe.transpose(T[:, t * 128:t * 128 + 128], norms.xn[:, s, t, :], core.ident[:, :])
                            ins.then_inc(TR.filled, 1)
                        elif kind in ("q", "k"):
                            if kind == "q":
                                wait(pe, *TR.emptying(k, ("xT",)))
                            wait(pe, *R.last(k, step))
                            pe.matmul(chunk[R.slot(step)][:, 0:512], W(f"w{kind}")[:, :], xnT[:, s, :],
                                      start=True, stop=True)
                            pe.matmul(chunk[R.slot(step)][:, 512:1024], W(f"w{kind}_swapped")[:, :],
                                             xnT[:, s, :], start=True, stop=True).then_inc(R.filled, 1)
                        elif kind == "v":
                            wait(pe, *R.last(k, step))
                            for t in range(tiles):
                                ins = pe.matmul(chunk[R.slot(step)][:, t * 128:t * 128 + 128],
                                                xnT[:, 1 - s, t * 128:t * 128 + 128], W("wv")[:, :],
                                                start=True, stop=True)
                            ins.then_inc(R.filled, 1)
                        elif kind == "y":
                            wait(pe, *TR.emptying(k, ("attT", 1)))
                            wait(pe, *R.last(k, step))
                            for t in range(tiles):
                                ins = pe.matmul(chunk[R.slot(step)][:, t * 128:t * 128 + 128],
                                                attT[:, t // 2, (t % 2) * 128:(t % 2) * 128 + 128], W("wo")[:, :],
                                                start=True, stop=True)
                            ins.then_inc(R.filled, 1)

                def block_is_this(i):
                    return not (i < STEPS.index(("half done",)) and STEPS[i][1] == 1)

                for signal, c in core.loaded(name):
                    pe.wait_ge(signal, c)
                bodies(pe, body)

            @block.scalar
            def _(eng):
                def body(n, s):
                    k = k_of(n)
                    if isinstance(n, int) and n == -1:
                        eng.wait_ge(stack_cleared, 1)
                    for i, step in enumerate(STEPS):
                        kind, b = step[0], step[1] if len(step) > 1 else None
                        if not present(n, i):
                            if kind == "exp":
                                R.skip_emptying(eng, k, step)
                            elif kind in ("xT", "maxT", "attT"):
                                TR.skip_emptying(eng, k, step)
                            elif kind == "pv" and step[2] % 2:
                                OR.skip_emptying(eng, k, step)
                            continue
                        if kind == "exp":
                            j = step[2]
                            wait(eng, *R.filling(k, step))
                            older = ("pv", b, (j - 4) // 2) if j >= 4 else ("pv", 1 - b, 2 + j // 2)
                            kk = k - 1 if b == 0 and j < 2 else k
                            if not (isinstance(n, int) and n == 0 and b == 0 and j < 4):
                                wait_pv(eng, kk, older)
                            eng.activation(P[:, j % 4, :, :, :],
                                                     chunk[R.slot(step)][:, :].rearrange("p (h k t) -> p h k t", h=2, k=2),
                                                     ACT.Exp, bias=core.zero[:, :], scale=SCALE).then_inc(R.emptied(step), 1)
                        elif kind == "pv" and step[2] % 2:
                            h = step[2] // 2
                            wait(eng, *OR.filling(k, step))
                            older = ("oT", 1 - b, h)
                            j = STEPS.index(older)
                            kk = k if j < i else k - 1
                            wait(eng, *TR.filling(kk, older))
                            eng.activation(O_sb[:, h, :, :], O[:, :, :], ACT.Copy).then_inc(OR.emptied(step), 1)
                        elif kind == "attT":
                            wait(eng, *TR.filling(k, step))
                            wait(eng, *R.filling(k if b == 0 else k - 1, ("y",)))
                            eng.activation(attT[:, b, :], T[:, 0:SEQ], ACT.Copy).then_inc(TR.emptied(step), 1)
                        elif kind == "maxT":
                            h = step[2]
                            wait(eng, *TR.filling(k, step))
                            m = block_of(n, i)
                            wait(eng, max_loaded[b][h], 16 * m)
                            eng.activation(M[:, b, h, :], T16[0:3 * HALF, 0:SEQ], ACT.Copy)\
                                .then_inc(TR.emptied(step), 1)
                            wait(eng, *TR.emptying(k, step))
                            eng.dma_start(stack[b][0][ROWS:ROWS + 3, h * HALF:h * HALF + HALF, :], M[:, b, h, :])\
                                .then_inc(max_loaded[b][h], 16)
                        elif kind == "xT":
                            wait(eng, *TR.filling(k, step))
                            if not (isinstance(n, int) and n == -2):
                                wait(eng, *R.filling(k - 1, ("v",)))
                            eng.activation(xnT[:, s, :], T[:, :], ACT.Copy).then_inc(TR.emptied(step), 1)
                            if isinstance(n, int) and n == -1:
                                for q in (1, 2, None):
                                    split_parts(-2, 0, q)
                        elif kind in ("part", "store"):
                            if not (isinstance(n, int) and n == -2 and b != 0):
                                split_parts(n, s, b)

                def split_parts(n, s, q):
                    m = n + 2
                    if q == 0:
                        eng.wait_ge(added, 2 * m + 2)
                        for b in range(2):
                            wait(eng, stored[b], 16 * m)
                    elif q is not None:
                        eng.wait_ge(rest_done, 2 * m + q)
                    if q is not None:
                        eng.activation(parts[:, :, q, :], qk[:, :, :], ACT.Copy).then_inc(part_done, 1)
                    else:
                        eng.wait_ge(part_done, 3 * m + 3)
                        if not (isinstance(n, int) and n < 0):
                            for b in range(2):
                                for h in range(2):
                                    eng.wait_ge(loaded[b][h], LOADS * (m - 1))
                        for b in range(2):
                            eng.dma_start(scratch[s, b, :, :, :].rearrange("q p t -> p q t"),
                                          parts[:, :, :, b * SEQ:b * SEQ + SEQ].rearrange("p x q t -> p (x q) t"))\
                               .then_inc(stored[b], 16)

                for signal, c in core.loaded(name):
                    eng.wait_ge(signal, c)
                bodies(eng, body)

            @block.sync
            def _(sp):
                core.weights.prefetch(sp, name)
                def load(n, s, b, h):
                    wait_apart(sp, stored[b], 16 * n + 16, core.sp_passed)
                    if not (isinstance(n, int) and n == 0):
                        wait(sp, *R.filling(n + 1, ("exp", b, 4 * h + 3)))
                    run, part = HALF * SEQ, D * SEQ
                    for x in range(2):
                        for i in range(3):
                            base = scratch.offset + ((s * 2 + b) * 6 + 3 * x + (0 if x == 0 else i)) * part + h * HD * run
                            which = [part, 3] if x == 0 else [0, 3]
                            sp.dma_start(stack[b][x][3 * HD * i:3 * HD * i + 3 * HD, h * HALF:h * HALF + HALF, :],
                                         bass.AP(scratch.tensor, base, [which, [1, HD * run]]))\
                                .then_inc(loaded[b][h], 16)
                    sp.dma_start(stack[b][0][ROWS:ROWS + 3, h * HALF:h * HALF + HALF, :], fixed[:, 0, :, :])\
                        .then_inc(loaded[b][h], 16)

                def body(n, s):
                    for b in range(2):
                        for h in range(2):
                            load(n, s, b, h)

                sp.wait_ge(stack_cleared, 1)
                sp.wait_ge(pool_cleared, 2)
                for b in range(2):
                    for h in range(2):
                        sp.dma_start(stack[b][1][ROWS:ROWS + 3, h * HALF:h * HALF + HALF, :], fixed[:, 1, :, :])\
                            .then_inc(ones_loaded, 16)
                blocks(sp, count, lambda n, s, first, last: body(n, s))
                for b in range(2):
                    sp.wait_ge(stored[b], 16 * (count + 1))
                if stage.last:
                    norms.store(sp)

            @block.vector
            def _(dve):
                def body(n, s):
                    k = k_of(n)
                    for i, step in enumerate(STEPS):
                        kind, b = step[0], step[1] if len(step) > 1 else None
                        if not present(n, i):
                            if kind in ring_of and kind != "exp":
                                R.skip_emptying(dve, k, step)
                            elif kind == "oT":
                                TR.skip_emptying(dve, k, step)
                                wait(dve, sums_done, k * 4 + oTs.index(step))
                                dve.sem_inc(sums_done, 1)
                            elif kind == "split":
                                wait(dve, split_step, k * 20 + 5 * splits.index(step))
                                dve.sem_inc(split_step, 5)
                            continue
                        if kind == "q" and isinstance(n, int) and n == -2:
                            clear_stacks()
                        if kind == "q" and isinstance(n, int) and n == -1:
                            clear_v()
                        if kind == "score":
                            c = step[2]
                            wait(dve, *R.filling(k, step))
                            src = chunk[R.slot(step)][:, :].rearrange("p (h t) -> p h t", h=4)
                            at = (c // 2) % 2 * 4
                            dve.tensor_reduce(nmax[:, b, c // 4, c % 2, at:at + 4], src, AX.X, ALU.max,
                                                        negate=True).then_inc(R.emptied(step), 1)
                        elif kind == "split":
                            h = step[2]
                            wait(dve, *R.emptying(k, ("score", b, 4 * h + 3)))
                            c = Chain(dve, split_step, k, 20)
                            c.j = 5 * splits.index(step)
                            part = lambda q: mparts[:, b, h, :, q, :]
                            c.link(dve.tensor_copy(part(0), nmax[:, b, h, :, :]))
                            c.link(dve.tensor_tensor(rest[:, :, :], nmax[:, b, h, :, :], part(0), ALU.subtract))
                            c.link(dve.tensor_copy(part(1), rest[:, :, :]))
                            c.link(dve.tensor_tensor(rest[:, :, :], rest[:, :, :], part(1), ALU.subtract))
                            c.link(dve.tensor_copy(part(2), rest[:, :, :]))
                        elif kind == "oT":
                            h = step[2]
                            wait(dve, *TR.filling(k, step))
                            groups = T[:, :].rearrange("p (a q d) -> p a q d", q=4, d=32)
                            dve.reciprocal(rsum[:, :, :], groups[:, :, :, HD]).then_inc(sums_done, 1)
                            dve.wait_ge(sums_done, k * 4 + oTs.index(step) + 1)
                            wait(dve, *TR.filling(k if step == ("oT", 1, 0) else k - 1, ("attT", b)))
                            src = T[:, :].rearrange("p (a x d) -> p a x d", a=2, d=32)
                            out = att[:, b, :, h * 64:h * 64 + 64].rearrange("p a (x d) -> p a x d", d=HD)
                            scale = rsum[:, :, :].rearrange("p (a g) q -> p a (g q)", a=2)\
                                .rearrange("p a (x o) -> p a x o", o=1).to_broadcast([128, 2, 8, HD])
                            dve.tensor_tensor(out, src[:, :, :, 0:HD], scale, ALU.mult).then_inc(TR.emptied(step), 1)
                        elif kind in ("q", "k"):
                            x = int(kind == "k")
                            wait(dve, *R.filling(k, step))
                            wait(dve, added, 2 * (n + 2) + x - 1)
                            src = chunk[R.slot(step)]
                            dve.scalar_tensor_tensor(rot[:, x, 0, :], src[:, 0:512], W(f"b{kind}")[:, :],
                                                     W("cos")[:, :], ALU.add, ALU.mult).then_inc(rope_done, 1)
                            dve.scalar_tensor_tensor(rot[:, x, 1, :], src[:, 512:1024],
                                                               W(f"b{kind}_swapped")[:, :], W("sin")[:, :],
                                                               ALU.add, ALU.mult).then_inc(R.emptied(step), 1)
                        elif kind == "v":
                            wait(dve, *R.filling(k, step))
                            wait(dve, *OR.filling(k, ("pv", 1, 3)))
                            bias = W("bv")[:, :].rearrange("p (o h d) -> p o h d", o=1, d=HD).to_broadcast([128, tiles, HEADS, HD])
                            dve.tensor_tensor(V32[:, 1 - s, :, :, 0:HD],
                                                        chunk[R.slot(step)][:, 0:512].rearrange("p (t h d) -> p t h d", t=tiles, d=HD),
                                                        bias, ALU.add).then_inc(R.emptied(step), 1)
                        elif kind == "y":
                            wait(dve, *R.filling(k, step))
                            dve.wait_ge(norms.yn_free, n + 1)
                            bias = W("bo")[:, :].rearrange("p (o f) -> p o f", o=1).to_broadcast([128, tiles, D])
                            dve.tensor_tensor(y[:, :, :], chunk[R.slot(step)][:, 0:512].rearrange("p (t f) -> p t f", t=tiles),
                                                        bias, ALU.add).then_inc(R.emptied(step), 1)
                            wait(dve, *R.emptying(k, step))
                            norms.post_statistics(dve, n - 1, 1 - s, y, None)
                        elif kind == "post":
                            norms.post_normalise(dve, n - 1, 1 - s, y)
                        elif kind == "stats":
                            norms.pre_statistics(dve, n + 2, s)
                        elif kind == "norm":
                            if not (isinstance(n, int) and n == -2):
                                wait(dve, *TR.filling(k - 1, ("xT",)))
                            norms.pre_normalise(dve, n + 2, s, None)

                def clear_stacks():
                    dve.memset(stack[0][0][64:96, :, :], 0.0)
                    dve.memset(stack[0][1][64:96, :, :], 0.0)
                    dve.memset(fixed[:, 0, :, :], 0.0).then_inc(stack_cleared, 1)

                def clear_v():
                    dve.memset(V32[:, :, :, :, :], 0.0).then_inc(v_cleared, 1)
                    dve.wait_ge(v_cleared, 1)
                    dve.memset(V32[:, :, :, :, HD:HD + 1], 1.0).then_inc(cleared, 1)
                    dve.wait_ge(cleared, 1)

                for signal, c in core.loaded(name):
                    dve.wait_ge(signal, c)
                bodies(dve, body)

            @block.gpsimd
            def _(pool):
                core.weights.prefetch_converted(pool, name)

                def body(n, s):
                    m = n + 2
                    has = not (isinstance(n, int) and m >= count)
                    if has:
                        if not (isinstance(n, int) and n == -1):
                            norms.pre_rstd(pool, m, s)
                        if isinstance(n, int) and n == -2:
                            pool.wait_ge(norms.pre_rstd_done, 1)
                            pool.memset(stack[1][0][64:96, :, :], 0.0)
                            pool.memset(stack[1][1][64:96, :, :], 0.0).then_inc(pool_cleared, 1)
                            pool.wait_ge(pool_cleared, 1)
                            pool.memset(fixed[:, 1, :, :], 1.0).then_inc(pool_cleared, 1)
                            pool.wait_ge(pool_cleared, 2)
                        for x in range(2):
                            wait(pool, *R.emptying(k_of(n), ("q",) if x == 0 else ("k",)))
                            wait(pool, part_done, 3 * m)
                            pool.tensor_tensor(qk[:, x, :], rot[:, x, 0, :], rot[:, x, 1, :], ALU.add).then_inc(added, 1)
                    if not (isinstance(n, int) and n < 1):
                        norms.post_rstd(pool, n - 1, 1 - s)
                        norms.add_to_x(pool, n - 1, 1 - s)
                    if isinstance(n, int) and n == -2:
                        norms.pre_rstd(pool, m + 1, 1 - s)
                    if has:
                        for q in range(2):
                            pool.wait_ge(part_done, 3 * m + q + 1)
                            pool.tensor_tensor(qk[:, :, :], qk[:, :, :], parts[:, :, q, :], ALU.subtract)\
                                .then_inc(rest_done, 1)

                pool.sem_inc(norms.yn_free, 2)
                bodies(pool, body)
        stage.clear()

def landmark_attention(nc, core):
    w, name, tiles, PAIRS, MARKS, ROUNDS = core.w, "L1a", ATT_TILES, HEADS // 2, 64, 6
    EACH = SEQ // MARKS
    W = lambda k: w[f"{name}_{k}"]
    INV = 3 * ROUNDS
    front = ("stats", "norm", "xT", "qk", "v", "means", "S3", "K3T", "S1", "sum1", "kc", "csum", "wT", "w", "S1T")
    back = ("z6T", "z6", "outT", "y", "post")
    AUX = {(0, 1): ["z0T", "stats", "z6T"], (1, 0): ["z6"], (1, 1): ["norm", "z0"], (2, 1): ["xT", "outT"],
           (3, 0): ["qk"], (3, 1): ["means"], (4, 0): ["y"], (5, 0): ["v"],
           (5, 1): [("S3", 0), ("S3", 1), "post"], (6, 0): [("S3", 2)], (6, 1): [("K3T", 0), ("S3", 3)],
           (7, 1): [("S3", 4)], (8, 0): [("S3", 5)], (8, 1): [("K3T", 1)], (9, 0): [("S3", 6), ("S3", 7)],
           (10, 0): [("S1", 0)], (10, 1): ["kc"], (11, 0): [("K3T", 2), ("S1", 1)],
           (11, 1): [("K3T", 3), ("sum1", 0)], (12, 0): ["csum"], (12, 1): [("S1", 2), ("sum1", 1)],
           (13, 0): ["wT"], (13, 1): [("S1", 3), ("sum1", 2), "w", ("S1T", 0)], (14, 1): [("sum1", 3)],
           (15, 0): [("S1T", 1)], (16, 0): [("S1T", 2)], (17, 0): [("S1T", 3)]}

    def steps():
        for j in range(INV):
            for g in range(2):
                yield ("inv", g, j)
                yield from (a if isinstance(a, tuple) else (a,) for a in AUX.get((j, g), ()))

    STEPS = list(steps())

    def present(n, step):
        if not isinstance(n, int):
            return True
        return step[0] in front and n + 1 < BATCHES or step[0] in back and n >= 1 or \
            step[0] not in front + back and 0 <= n < BATCHES

    def bodies(eng, body):
        body(-1, 1)
        body(0, 0)
        with eng.Fori(0, (BATCHES - 2) // 2) as i:
            body(2 * i + 1, 1)
            body(2 * i + 2, 0)
        body(BATCHES - 1, 1)
        body(BATCHES, 0)

    with ExitStack() as ctx:
        stage = Stage(nc, ctx, core, name)
        sb, sem, bank = stage.sbuf, stage.sem, stage.bank
        norms = Norms(nc, core, stage, tiles)
        xnT, qT, kk = sb("xnT", [128, SEQ]), sb("qT", [128, SEQ]), sb("k_and_landmarks", [128, SEQ + MARKS])
        sums, ql = sb("sums", [128, 2, MARKS]), sb("ql", [128, MARKS])
        klm, qlm = sb("kl_by_head", [128, HEADS, MARKS]), sb("ql_by_head", [128, HEADS, MARKS])
        vx, wx, zx, w2x = (sb(n, s) for n, s in (("v_spaced", [128, tiles, 4, 48]), ("w_spaced", [128, 4, 48]),
                                                 ("z_spaced", [128, 4, 48]), ("result_spaced", [128, 4, 48])))
        P1, P1T = sb("prob1", [128, 4, 512]), sb("prob1T", [128, 2, PAIRS, SEQ])
        P3, P3T = sb("exp3", [128, 4, SEQ]), sb("exp3T", [128, tiles, PAIRS, 128])
        P2, Kc, Kbd = sb("exp2", [128, PAIRS, MARKS]), sb("K", [128, PAIRS, MARKS]), sb("K_diagonal", [128, PAIRS, 128])
        nmax1, inv1 = sb("max1", [128, 4, 8]), sb("inv_sum1", [128, 4, 8])
        nmax3, nmax2 = sb("neg_max3", [128, PAIRS]), sb("neg_max2", [128, PAIRS])
        sum3, sum2 = sb("sum3", [128, PAIRS]), sb("sum2", [128, PAIRS])
        inv3, inv2, den = sb("inv_sum3", [128, PAIRS]), sb("inv_sum2", [128, PAIRS]), sb("denominator", [128, PAIRS])
        invd = sb("inv_denominator", [128, PAIRS])
        wT_sb, z0T_sb, z6T_sb, oT = sb("wT", [128, 128]), sb("z0T", [128, 128]), sb("z6T", [128, 128]), sb("oT", [128, SEQ])
        AZ, E = sb("7A_and_z", [128, PAIRS, 144]), sb("15_less_7A", [128, PAIRS, 128])
        C, Dm = sb("C", [128, PAIRS, 128]), sb("D_quarter", [128, PAIRS, 128])
        y = sb("y", [128, tiles, D])
        G = [bank(f"G{g}", [128, 2, 512]) for g in range(2)]
        F = [bank(f"F{i}", [128, 512]) for i in range(4)]

        emptied_by = {"z6T": "act", "z0T": "act", "z6": "dve", "z0": "dve", "outT": "act", "xT": "act", "qk": "act", "y": "act",
                  "v": "act", "S3": "act", "K3T": "act", "S1": "dve", "csum": "dve", "wT": "act", "w": "dve", "S1T": "act"}
        R = Turns(stage, "F", 4, [(s, emptied_by[s[0]]) for s in STEPS if s[0] in emptied_by])
        of = lambda step: F[R.slot(step)]
        full, read = [sem(f"G{g}_full") for g in range(2)], [sem(f"G{g}_read") for g in range(2)]
        e_done = [sem(f"E{g}_done") for g in range(2)]
        sums_done, ql_done, kl_done, heads_done = sem("sums_done"), sem("ql_done"), sem("kl_done"), sem("heads_done")
        max_done, exp3_done, exp2_done = sem("max_done"), sem("exp3_done"), sem("exp2_done")
        max1_done, sub_done, exp1_done, sum1_done = sem("max1_done"), sem("sub_done"), sem("exp1_done"), sem("sum1_done")
        inv1_done, prob1_done, inv2_done, kc_done = sem("inv1_done"), sem("prob1_done"), sem("inv2_done"), sem("kc_done")
        diagonal_done, den_done, invd_done, cleared = sem("diagonal_done"), sem("den_done"), sem("invd_done"), sem("cleared")

        def spaced(buf):
            return buf.rearrange("p j (c f) -> p j c f", f=16)[:, :, 0:3:2, :]

        def by_pair(a):
            return a.rearrange("p (j c f) -> p j c f", j=4, c=2)

        def wide(buf, pair):
            j, c = pair // 2, pair % 2
            return buf[:, j, 16 * c:16 * c + 32]

        def over(a, inner):
            return a.rearrange("p (k o) -> p k o", o=1).to_broadcast([a.shape[0], a.shape[1], inner])

        def matrix(a, k):
            return a.rearrange("p (o f) -> p o f", o=1).to_broadcast([128, k, a.shape[1]])

        with nc.Block() as block:
            @block.tensor
            def _(pe):
                def inverse(n, g, j):
                    if j == 0:
                        pe.wait_ge(diagonal_done, n + 1)
                    wait(pe, read[g], INV * n + j)
                    r, s = (j - 1) // 3, (j - 1) % 3
                    for q in range(4):
                        p = 4 * g + q
                        A = AZ[:, p, 0:128]
                        if j > 0 and s == 2:
                            out, lhsT, rhs = G[g][:, q // 2, q % 2 * 144:q % 2 * 144 + 144], Dm[:, p, :], AZ[:, p, :]
                        else:
                            out = G[g][:, 0, q * 128:q * 128 + 128]
                            lhsT, rhs = (Kbd[:, p, :], Kbd[:, p, :]) if j == 0 else (A, A) if s == 0 else (A, C[:, p, :])
                        ins = pe.matmul(out, lhsT, rhs, start=True, stop=True)
                    ins.then_inc(full[g], 1)

                def columns(step, spaced_operand, operands):
                    width = operands(0).shape[-1]
                    for c in range(2):
                        for j in range(4):
                            ins = pe.matmul(of(step)[32 * j:32 * j + 32, 0:width], wide(spaced_operand, 2 * j + c),
                                            operands(2 * j + c), start=c == 0, stop=c == 1, tile_position=(0, 32 * j))
                    return ins

                def body(n, s):
                    k, m = n + 1, n + 1
                    for step in STEPS:
                        kind = step[0]
                        if not present(n, step):
                            if kind in emptied_by:
                                R.skip_filling(pe, k, step)
                            continue
                        if kind == "inv":
                            inverse(n, step[1], step[2])
                            continue
                        if kind not in emptied_by:
                            continue
                        wait(pe, *R.last(k, step))
                        out = of(step)
                        if kind == "z6T":
                            for g in range(2):
                                pe.wait_ge(read[g], INV * n)
                            ins = columns(step, zx, lambda p: Dm[:, p, :])
                        elif kind == "z0T":
                            wait(pe, *R.emptying(k - 1, ("w",)))
                            ins = columns(step, wx, lambda p: Kbd[:, p, :])
                        elif kind == "z6":
                            wait(pe, *R.emptying(k, ("z6T",)))
                            ins = pe.transpose(out[:, 0:128], z6T_sb[:, :], core.ident[:, :])
                        elif kind == "z0":
                            wait(pe, *R.emptying(k, ("z0T",)))
                            ins = pe.transpose(out[:, 0:128], z0T_sb[:, :], core.ident[:, :])
                        elif kind == "outT":
                            wait(pe, *R.emptying(k, ("z6",)))
                            ins = columns(step, w2x, lambda p: P1T[:, 1 - s, p, :])
                        elif kind == "y":
                            wait(pe, *R.emptying(k, ("outT",)))
                            for t in range(tiles):
                                ins = pe.matmul(out[:, t * 128:t * 128 + 128], oT[:, t * 128:t * 128 + 128],
                                                W("proj")[:, :], start=True, stop=True)
                        elif kind == "xT":
                            pe.wait_ge(norms.xn_done, m + 1)
                            for t in range(tiles):
                                ins = pe.transpose(out[:, t * 128:t * 128 + 128], norms.xn[:, 1 - s, t, :], core.ident[:, :])
                        elif kind == "qk":
                            wait(pe, *R.emptying(k, ("xT",)))
                            for x in range(2):
                                ins = pe.matmul(out[:, x * SEQ:x * SEQ + SEQ], W("qkv")[:, x * 128:x * 128 + 128],
                                                xnT[:, :], start=True, stop=True)
                        elif kind == "v":
                            for t in range(tiles):
                                ins = pe.matmul(out[:, t * 128:t * 128 + 128], xnT[:, t * 128:t * 128 + 128],
                                                W("qkv")[:, 256:384], start=True, stop=True)
                        elif kind == "S3":
                            p = step[1]
                            if p == 0:
                                pe.wait_ge(heads_done, 2 * m + 1)
                                pe.wait_ge(kl_done, m + 1)
                            ins = pe.matmul(out[:, 0:SEQ + MARKS], qlm[:, 2 * p:2 * p + 2, :], kk[:, :], start=True, stop=True)
                        elif kind == "K3T":
                            pe.wait_ge(exp3_done, 8 * m + 2 * step[1] + 2)
                            for q in range(2):
                                for t in range(tiles):
                                    at = (2 * t + q) * 128
                                    ins = pe.transpose(out[:, at:at + 128],
                                                       P3[:, (2 * step[1] + q) % 4, t * 128:t * 128 + 128], core.ident[:, :])
                        elif kind == "S1":
                            t, half = step[1] // 2, step[1] % 2
                            if step[1] == 0:
                                pe.wait_ge(heads_done, 2 * m + 2)
                            ins = pe.matmul(out[:, :], qT[:, t * 128:t * 128 + 128], klm[:, 8 * half:8 * half + 8, :],
                                            start=True, stop=True)
                        elif kind == "S1T":
                            pe.wait_ge(prob1_done, 4 * m + step[1] + 1)
                            for q in range(4):
                                ins = pe.transpose(out[:, q * 128:q * 128 + 128], P1[:, step[1], q * 128:q * 128 + 128],
                                                   core.ident[:, :])
                        elif kind == "csum":
                            pe.wait_ge(kc_done, m + 1)
                            ins = pe.matmul(out[:, :], W("ones")[:, :], Kc[:, :, :], start=True, stop=True)
                        elif kind == "wT":
                            wait(pe, *R.emptying(k, ("K3T", 3)))
                            for i in range(4):
                                c, t = i % 2, i // 2
                                for j in range(4):
                                    ins = pe.matmul(out[32 * j:32 * j + 32, 0:128], wide(vx[:, t, :, :], 2 * j + c),
                                                    P3T[:, t, 2 * j + c, :], start=i == 0, stop=i == 3,
                                                    tile_position=(0, 32 * j))
                        elif kind == "w":
                            wait(pe, *R.emptying(k, ("wT",)))
                            ins = pe.transpose(out[:, 0:128], wT_sb[:, :], core.ident[:, :])
                        ins.then_inc(R.filled, 1)

                for signal, c in core.loaded(name):
                    pe.wait_ge(signal, c)
                pe.wait_ge(cleared, 1)
                bodies(pe, body)

            @block.sync
            def _(sp):
                core.weights.prefetch(sp, name)
                if stage.last:
                    norms.store(sp)

            @block.scalar
            def _(eng):
                copy = lambda out, src, scale=1.0: eng.activation(out, src, ACT.Copy, scale=scale)

                def body(n, s):
                    k, m = n + 1, n + 1
                    for step in STEPS:
                        kind = step[0]
                        if not present(n, step):
                            if emptied_by.get(kind) == "act":
                                R.skip_emptying(eng, k, step)
                            continue
                        if kind == "inv":
                            g, j = step[1:]
                            if j > 0 and (j - 1) % 3 == 2:
                                eng.wait_ge(full[g], INV * n + j + 1)
                                both = G[g][:, :, 0:288].rearrange("p b (q f) -> p b q f", q=2)
                                dest = AZ[:, 4 * g:4 * g + 4, :].rearrange("p (b q) f -> p b q f", b=2)
                                if j == INV - 3:
                                    copy(spaced(zx[:, 2 * g:2 * g + 2, :]), both[:, :, :, 128:144])
                                    ins = copy(dest[:, :, :, 0:128], both[:, :, :, 0:128])
                                else:
                                    ins = copy(dest, both)
                                ins.then_inc(read[g], 1)
                            continue
                        if emptied_by.get(kind) == "act":
                            wait(eng, *R.filling(k, step))
                        src = of(step) if kind in emptied_by else None
                        if kind in ("z6T", "z0T", "wT"):
                            to = {"z6T": z6T_sb, "z0T": z0T_sb, "wT": wT_sb}[kind]
                            copy(to[:, :], src[:, 0:128]).then_inc(R.emptied(step), 1)
                        elif kind in ("outT", "xT"):
                            copy({"outT": oT, "xT": xnT}[kind][:, :], src[:, 0:SEQ]).then_inc(R.emptied(step), 1)
                        elif kind == "y":
                            wait(eng, norms.yn_done, n - 1)
                            copy(y[:, :, :], src[:, 0:SEQ].rearrange("p (t f) -> p t f", t=tiles))\
                                .then_inc(R.emptied(step), 1)
                        elif kind == "qk":
                            copy(qT[:, :], src[:, 0:SEQ], 1.0 / float(np.sqrt(np.float32(HD))))
                            copy(kk[:, 0:SEQ], src[:, SEQ:]).then_inc(R.emptied(step), 1)
                        elif kind == "v":
                            for t in range(tiles):
                                ins = copy(spaced(vx[:, t, :, :]), by_pair(src[:, t * 128:t * 128 + 128]))
                            ins.then_inc(R.emptied(step), 1)
                        elif kind == "S3":
                            p = step[1]
                            eng.wait_ge(max_done, 8 * m + p + 1)
                            if p >= 4:
                                wait(eng, *R.filling(k, ("K3T", (p - 4) // 2)))
                            elif not (isinstance(n, int) and n < 0):
                                wait(eng, *R.filling(k - 1, ("K3T", (p + 4) // 2)))
                            eng.activation(P3[:, p % 4, :], src[:, 0:SEQ], ACT.Exp, bias=nmax3[:, p:p + 1],
                                           accum_out=sum3[:, p:p + 1]).then_inc(exp3_done, 1)
                            eng.activation(P2[:, p, :], src[:, SEQ:SEQ + MARKS], ACT.Exp,
                                                     bias=nmax2[:, p:p + 1], accum_out=sum2[:, p:p + 1]).then_inc(R.emptied(step), 1)
                        elif kind == "K3T":
                            q = 2 * step[1]
                            copy(P3T[:, :, q:q + 2, :], src[:, :].rearrange("p (t q f) -> p t q f", t=2, q=2)).then_inc(R.emptied(step), 1)
                        elif kind == "sum1":
                            c = step[1]
                            eng.wait_ge(sub_done, 4 * m + c + 1)
                            eng.activation(P1[:, c, :], P1[:, c, :], ACT.Exp, bias=core.zero[:, :]).then_inc(exp1_done, 1)
                        elif kind == "csum":
                            eng.wait_ge(kc_done, m + 1)
                            if not (isinstance(n, int) and n < 0):
                                wait(eng, *R.filling(k, ("z0T",)))
                            for hh in range(2):
                                ins = copy(Kbd[64 * hh:64 * hh + 64, :, 64 * hh:64 * hh + 64],
                                           Kc[64 * hh:64 * hh + 64, :, :])
                            ins.then_inc(diagonal_done, 1)
                        elif kind == "S1T":
                            t, half = step[1] // 2, step[1] % 2
                            copy(P1T[:, 1 - s, 4 * half:4 * half + 4, t * 128:t * 128 + 128],
                                           src[:, :].rearrange("p (q f) -> p q f", q=4)).then_inc(R.emptied(step), 1)

                for signal, c in core.loaded(name):
                    eng.wait_ge(signal, c)
                eng.wait_ge(cleared, 1)
                bodies(eng, body)

            @block.vector
            def _(dve):
                def body(n, s):
                    k, m = n + 1, n + 1
                    for step in STEPS:
                        kind = step[0]
                        if not present(n, step):
                            if emptied_by.get(kind) == "dve":
                                R.skip_emptying(dve, k, step)
                            continue
                        if kind == "inv":
                            g, j = step[1:]
                            r, at = (j - 1) // 3, slice(4 * g, 4 * g + 4)
                            src = G[g][:, 0, :].rearrange("p (q f) -> p q f", q=4)
                            if j == 0:
                                dve.wait_ge(invd_done, n + 1)
                                dve.wait_ge(full[g], INV * n + 1)
                                dve.scalar_tensor_tensor(AZ[:, at, 0:128], src, 7.0, over(invd[:, at], 128),
                                                         ALU.mult, ALU.mult)\
                                    .then_inc(read[g], 1)
                            elif (j - 1) % 3 == 0:
                                dve.wait_ge(e_done[g], ROUNDS * n + r + 1)
                                dve.wait_ge(full[g], INV * n + j + 1)
                                dve.scalar_tensor_tensor(C[:, at, :], src, 1.0 / 49.0, E[:, at, :], ALU.mult, ALU.add)\
                                    .then_inc(read[g], 1)
                            elif (j - 1) % 3 == 1:
                                dve.wait_ge(full[g], INV * n + j + 1)
                                dve.scalar_tensor_tensor(Dm[:, at, :], src, -0.25 / 7.0, matrix(W("thirteen_quarters")[:, :], 4),
                                                         ALU.mult, ALU.add).then_inc(read[g], 1)
                            continue
                        if emptied_by.get(kind) == "dve":
                            wait(dve, *R.filling(k, step))
                        src = of(step) if kind in emptied_by else None
                        if kind == "z6":
                            dve.tensor_tensor(spaced(w2x[:, :, :]), by_pair(src[:, 0:128]),
                                                        by_pair(W("own_head")[:, :]), ALU.mult).then_inc(R.emptied(step), 1)
                        elif kind == "z0":
                            dve.wait_ge(invd_done, n + 1)
                            dve.tensor_tensor(AZ[:, :, 128:144], src[:, 0:128].rearrange("p (k f) -> p k f", k=PAIRS),
                                                        over(invd[:, :], 16), ALU.mult).then_inc(R.emptied(step), 1)
                        elif kind == "w":
                            dve.wait_ge(inv2_done, 2 * m + 2)
                            dve.tensor_tensor(spaced(wx[:, :, :]), by_pair(src[:, 0:128]),
                                                        over(inv3[:, :], 16).rearrange("p (j c) f -> p j c f", j=4),
                                                        ALU.mult).then_inc(R.emptied(step), 1)
                        elif kind == "means":
                            wait(dve, *R.emptying(k, ("qk",)))
                            dve.tensor_reduce(sums[:, 0, :], qT[:, :].rearrange("p (m e) -> p m e", e=EACH), AX.X, ALU.add)
                            dve.tensor_reduce(sums[:, 1, :], kk[:, 0:SEQ].rearrange("p (m e) -> p m e", e=EACH), AX.X, ALU.add)\
                                .then_inc(sums_done, 1)
                            dve.wait_ge(sums_done, m + 1)
                            dve.tensor_scalar(ql[:, :], sums[:, 0, :], 1.0 / EACH, None, ALU.mult).then_inc(ql_done, 1)
                            dve.tensor_scalar(kk[:, SEQ:], sums[:, 1, :], 1.0 / EACH, None, ALU.mult).then_inc(kl_done, 1)
                        elif kind == "S3":
                            p = step[1]
                            wait(dve, *R.filling(k, step))
                            dve.tensor_reduce(nmax3[:, p:p + 1], src[:, 0:SEQ], AX.X, ALU.max, negate=True)
                            dve.tensor_reduce(nmax2[:, p:p + 1], src[:, SEQ:SEQ + MARKS], AX.X, ALU.max, negate=True)\
                                .then_inc(max_done, 1)
                        elif kind == "S1":
                            c = step[1]
                            logits = src[:, :].rearrange("p (h m) -> p h m", h=8)
                            dve.tensor_reduce(nmax1[:, c, :], logits, AX.X, ALU.max).then_inc(max1_done, 1)
                            dve.wait_ge(max1_done, 4 * m + c + 1)
                            ins = dve.tensor_tensor(P1[:, c, :].rearrange("p (h m) -> p h m", h=8), logits,
                                                    over(nmax1[:, c, :], MARKS), ALU.subtract)
                            ins.then_inc(R.emptied(step), 1)
                            dve.wait_ge(*R.emptying(k, step))
                            dve.sem_inc(sub_done, 1)
                        elif kind == "sum1":
                            c = step[1]
                            dve.wait_ge(exp1_done, 4 * m + c + 1)
                            dve.tensor_reduce(inv1[:, c, :], P1[:, c, :].rearrange("p (h m) -> p h m", h=8), AX.X, ALU.add)\
                                .then_inc(sum1_done, 1)
                            dve.wait_ge(sum1_done, 4 * m + c + 1)
                            dve.reciprocal(inv1[:, c, :], inv1[:, c, :]).then_inc(inv1_done, 1)
                        elif kind == "kc":
                            wait(dve, *R.emptying(k, ("S3", PAIRS - 1)))
                            dve.reciprocal(inv2[:, :], sum2[:, :]).then_inc(inv2_done, 1)
                            dve.reciprocal(inv3[:, :], sum3[:, :]).then_inc(inv2_done, 1)
                            dve.wait_ge(inv2_done, 2 * m + 1)
                            dve.tensor_tensor(Kc[:, :, :], P2[:, :, :], over(inv2[:, :], MARKS), ALU.mult).then_inc(kc_done, 1)
                        elif kind == "csum":
                            dve.tensor_reduce(den[:, :], src[:, :].rearrange("p (k m) -> p k m", k=PAIRS),
                                                        AX.X, ALU.max).then_inc(R.emptied(step), 1)
                            dve.wait_ge(*R.emptying(k, step))
                            dve.reciprocal(invd[:, :], den[:, :]).then_inc(invd_done, 1)
                        elif kind == "stats":
                            norms.pre_statistics(dve, m, 1 - s)
                        elif kind == "norm":
                            if not (isinstance(n, int) and n < 1):
                                wait(dve, *R.filling(k - 1, ("xT",)))
                            norms.pre_normalise(dve, m, 1 - s, None)
                        elif kind == "post":
                            wait(dve, *R.emptying(k, ("y",)))
                            norms.post_statistics(dve, n - 1, 1 - s, y, None)
                            norms.post_normalise(dve, n - 1, 1 - s, y)

                for signal, c in core.loaded(name):
                    dve.wait_ge(signal, c)
                bodies(dve, body)

            @block.gpsimd
            def _(pool):
                core.weights.prefetch_converted(pool, name)

                def body(n, s):
                    k, m = n + 1, n + 1
                    for step in STEPS:
                        kind = step[0]
                        if not present(n, step):
                            continue
                        if kind == "inv":
                            g, j = step[1:]
                            if j % 3 == 0 and j < INV:
                                pool.wait_ge(read[g], INV * n + j + 1)
                                pool.tensor_tensor(E[:, 4 * g:4 * g + 4, :], matrix(W("fifteen")[:, :], 4),
                                                   AZ[:, 4 * g:4 * g + 4, 0:128], ALU.subtract)\
                                    .then_inc(e_done[g], 1)
                        elif kind == "stats":
                            norms.pre_rstd(pool, m, 1 - s)
                        elif kind == "means":
                            if not (isinstance(n, int) and n < 0):
                                wait(pool, *R.filling(k - 1, ("S1", 3)))
                            for buf, src, signal, c in ((qlm, ql[:, :], ql_done, 0), (klm, kk[:, SEQ:], kl_done, 1)):
                                pool.wait_ge(signal, m + 1)
                                pool.tensor_tensor(buf[:, :, :], matrix(src, HEADS), over(W("heads")[:, :], MARKS), ALU.mult)\
                                    .then_inc(heads_done, 1)
                        elif kind == "sum1":
                            c = step[1]
                            pool.wait_ge(inv1_done, 4 * m + c + 1)
                            rows = P1[:, c, :].rearrange("p (h m) -> p h m", h=8)
                            pool.tensor_tensor(rows, rows, over(inv1[:, c, :], MARKS), ALU.mult).then_inc(prob1_done, 1)
                        elif kind == "post":
                            norms.post_rstd(pool, n - 1, 1 - s)
                            norms.add_to_x(pool, n - 1, 1 - s)

                pool.sem_inc(norms.yn_free, 2)
                for buf in (vx, wx, zx, w2x, Kbd):
                    ins = pool.memset(buf[tuple([slice(None)] * len(buf.shape))], 0.0)
                ins.then_inc(cleared, 1)
                for signal, c in core.loaded(name):
                    pool.wait_ge(signal, c)
                pool.wait_ge(cleared, 1)
                bodies(pool, body)
        stage.clear()

def lay_out(a):
    f = np.float32
    w = {}
    c = lambda x: np.ascontiguousarray(x)
    col = lambda v: c(v.reshape(-1, 1))
    row = lambda v: c(np.broadcast_to(v.reshape(1, -1), (128, v.size)))
    chunks = lambda m: c(m.reshape(-1, 128, m.shape[-1]).transpose(1, 0, 2))
    w["ident"] = np.eye(128, dtype=f)
    for k in ("wq", "wk", "wv", "wo"):
        w[f"L0a_{k}"] = c(a[f"L0_attn_{k}"])
    w["L0a_bq"], w["L0a_bk"] = col(a["L0_attn_bq"]), col(a["L0_attn_bk"])
    w["L0a_bv"], w["L0a_bo"] = row(a["L0_attn_bv"]), row(a["L0_attn_bo"])
    query = np.arange(SEQ).reshape(2, 128).T[:, :, None]
    keep = (np.arange(SEQ)[None, None, :] > query + 1).astype(f)
    w["L0a_keep"], w["L0a_never"] = keep, np.where(keep > 0, f(0), f(-1e9))
    w["L0f_gate"], w["L0f_up"] = c(a["L0_ffn_w_gate"].T), c(a["L0_ffn_w_up"].T)
    w["L0f_down"] = chunks(a["L0_ffn_w_down"].T)
    w["L1a_qkv"], w["L1a_proj"] = c(a["L1_attn_w_qkv"]), c(a["L1_attn_w_proj"])
    row_head = np.arange(128)[:, None] // 64
    w["L1a_heads"] = (np.arange(128)[:, None] // HD == np.arange(HEADS)).astype(f)
    w["L1a_ones"] = (row_head == np.arange(128) // 64).astype(f)
    w["L1a_own_head"] = (row_head == np.arange(128) % 16 // HD).astype(f)
    w["L1a_fifteen"], w["L1a_thirteen_quarters"] = 15 * np.eye(128, dtype=f), f(3.25) * np.eye(128, dtype=f)
    w["L1f_router"], w["L1f_router_b"] = c(a["L1_ffn_router_w"]), row(a["L1_ffn_router_b"])
    w["L1f_w1"] = c(a["L1_ffn_w1"].transpose(1, 0, 2).reshape(128, 2048))
    w["L1f_b1"] = c(a["L1_ffn_b1"].reshape(16, 128).T)
    w["L1f_w2"] = chunks(a["L1_ffn_w2"].reshape(2048, 128))
    w["L1f_b2"] = c(np.tile(a["L1_ffn_b2"].reshape(2, 32, 128), (1, 3, 1)).transpose(1, 0, 2))
    w["L1f_sw1"] = c(a["L1_ffn_sw1"].transpose(1, 0, 2).reshape(128, 512))
    w["L1f_sb1"] = c(a["L1_ffn_sb1"].reshape(4, 128).T)
    w["L1f_sw2"] = chunks(a["L1_ffn_sw2"].reshape(512, 128))
    w["L1f_sb2"] = c(a["L1_ffn_sb2"].T)
    part_row, expert_of = np.arange(96) % 32, np.arange(128) // 32
    w["L1f_select"] = c(np.stack([(part_row[:, None] == 4 * q + expert_of).astype(f) for q in range(8)], 1))
    d_of, h_of = np.arange(128) % 64 // 8, np.arange(128) // 64 * 8 + np.arange(128) % 8
    order, swapped = h_of * HD + d_of, h_of * HD + (d_of ^ 1)
    inverse = f(1.0) / f(10000.0) ** (np.arange(0, HD, 2, dtype=f) / f(HD))
    t = np.arange(SEQ, dtype=f)
    for n, which, m in (("L2a", d_of % 4, lambda v: v.T), ("L3a", d_of // 2 * 2 % 4, lambda v: v)):
        src = f"{n[:2]}_attn"
        for k in "qk":
            weights, bias = m(a[f"{src}_W{k}"]), a[f"{src}_b{k}"]
            w[f"{n}_w{k}"], w[f"{n}_w{k}_swapped"] = c(weights[:, order]), c(weights[:, swapped])
            w[f"{n}_b{k}"], w[f"{n}_b{k}_swapped"] = col(bias[order]), col(bias[swapped])
        w[f"{n}_wv"], w[f"{n}_wo"] = c(m(a[f"{src}_Wv"])), c(m(a[f"{src}_Wo"]))
        w[f"{n}_bv"], w[f"{n}_bo"] = row(a[f"{src}_bv"]), row(a[f"{src}_bo"])
        angle = inverse[which][:, None] * t[None, :]
        w[f"{n}_cos"] = np.tile(np.cos(angle), (1, 2)).astype(f)
        w[f"{n}_sin"] = np.tile(np.sin(angle) * np.where(d_of % 2 == 0, f(-1), f(1))[:, None], (1, 2)).astype(f)
    w["L2f_router"], w["L2f_router_b"] = c(a["L2_ffn_gate_w"].T), row(a["L2_ffn_gate_bias"])
    for name, shared in (("w1", "ws1"), ("w3", "ws3")):
        w[f"L2f_{name}"] = c(np.concatenate([a[f"L2_ffn_{name}"].reshape(1536, 128), a[f"L2_ffn_{shared}"]]).T)
    w["L2f_w2"] = chunks(a["L2_ffn_w2"].transpose(0, 2, 1).reshape(1536, 128))
    w["L2f_ws2"] = c(a["L2_ffn_ws2"].T)
    part_row = np.where(np.arange(128) < 48, np.arange(128) % 16, -1)
    w["L2f_select"] = c(np.stack([(part_row[:, None] == (128 * q + np.arange(128)) // 96).astype(f)
                                  for q in range(12)], 1))
    w["L3f_w1"], w["L3f_w2"] = c(a["L3_ffn_w1_w"].T), c(a["L3_ffn_w2_w"].T)
    w["L3f_h1"], w["L3f_h2"], w["L3f_w3"] = (chunks(a[f"L3_ffn_{k}_w"].T) for k in ("h1", "h2", "w3"))
    for k in ("w1", "w2", "h1", "h2", "w3"):
        w[f"L3f_{k}_s"] = c(a[f"L3_ffn_{k}_s"].reshape(-1, 128).T)
    return w


CONVERTED = {"L0f_gate": F32, "L0f_up": F32, "L0f_down": F32, "L1f_select": BF16, "L2f_select": BF16}


class Weights:

    def __init__(self, core, ctx, given, stages):
        self.given, self.stages, self.views, self.counts = given, stages, {}, {}
        names = {s: [n for n in given if n.startswith(s + "_")] for s in stages}
        dtype = lambda n: CONVERTED.get(n, given[n].dtype)
        size = lambda n: int(np.prod(given[n].shape[1:])) * (2 if dtype(n) == BF16 else 4) // 4
        for kind in "af":
            own = [s for s in stages if s[2] == kind]
            if not own:
                continue
            area = core.sbuf("attention_weights" if kind == "a" else "ffn_weights",
                             [128, max(sum(size(n) for n in names[s]) for s in own)])
            for s in own:
                at = 0
                for n in names[s]:
                    shape, w = given[n].shape, size(n)
                    view = area[0:shape[0], at:at + w]
                    if dtype(n) != F32:
                        view = view.bitcast(dtype(n))
                    if len(shape) == 3:
                        view = view.rearrange("p (a b) -> p a b", a=shape[1])
                    self.views[n], at = view, at + w
        self.names = names
        self.arrived, self.converted = ({s: ctx.enter_context(core.nc.semaphore(f"{s}_{n}")) for s in stages}
                                        for n in ("weights", "converted"))

    def loaded(self, s):
        n = [sum((name in CONVERTED) == c for name in self.names[s]) for c in (False, True)]
        return [(sem, 16 * k) for sem, k in ((self.arrived[s], n[0]), (self.converted[s], n[1])) if k]

    def load(self, sp, s):
        for n in self.names[s]:
            if n not in CONVERTED:
                sp.dma_start(self.views[n], self.given[n]).then_inc(self.arrived[s], 16)

    def load_converted(self, pool, s):
        for n in self.names[s]:
            if n in CONVERTED:
                pool.dma_start(self.views[n], self.given[n]).then_inc(self.converted[s], 16)

    def following(self, s):
        i = self.stages.index(s)
        return self.stages[i + 1] if 1 <= i < len(self.stages) - 1 else None

    def prefetch(self, sp, s):
        if self.following(s):
            self.load(sp, self.following(s))

    def prefetch_converted(self, pool, s):
        if self.following(s):
            self.load_converted(pool, self.following(s))


def ffn0(nc, core):
    w = core.w
    items = [Item(128, ACT.Silu, k, gate=w["L0f_gate"][:, 128 * k:128 * k + 128],
                  up=w["L0f_up"][:, 128 * k:128 * k + 128]) for k in range(3)]

    def dequantise(dve, stage):
        for n in ("L0f_gate", "L0f_up", "L0f_down"):
            v = w[n][tuple([slice(None)] * len(w[n].shape))]
            ins = dve.tensor_scalar(v, v, float(np.float32(1.0 / 127.0)), None, ALU.mult)
        return ins

    ffn_stage(nc, core, "L0f", items, [(w["L0f_down"][:, k, :], k) for k in range(3)],
              dict(post=0, pre=2, statistics=0, normalise=0), core.loaded("L0f"), prepare=dequantise)


def ffn1(nc, core):
    w = core.w
    items = [Item(128, ACT.Silu, k, gate=w["L1f_sw1"][:, 128 * k:128 * k + 128], bias=w["L1f_sb1"][:, k:k + 1])
             for k in range(4)]
    items += [Item(128, ACT.Silu, k % 4, gate=w["L1f_w1"][:, 128 * k:128 * k + 128], bias=w["L1f_b1"][:, k:k + 1],
                   expert=(w["L1f_select"][0:96, k % 8, :], k // 8)) for k in range(16)]
    down = [(w["L1f_sw2"][:, k, :], k) for k in range(4)] + [(w["L1f_w2"][:, k, :], 4 + k) for k in range(16)]
    b2 = core.sbuf("L1f_b2_parts", [96, 2, 3, 128], BF16)
    rest = core.sbuf("L1f_b2_rest", [96, 2, 128])
    sb2 = core.sbuf("L1f_sb2_sum", [128, 1])

    def prepare(dve, stage):
        step = stage.sem("b2_split")
        c = Chain(dve, step, 0, 5)
        c.link(dve.tensor_copy(b2[:, :, 0, :], w["L1f_b2"][:, :, :]))
        c.link(dve.tensor_tensor(rest[:, :, :], w["L1f_b2"][:, :, :], b2[:, :, 0, :], ALU.subtract))
        c.link(dve.tensor_copy(b2[:, :, 1, :], rest[:, :, :]))
        c.link(dve.tensor_tensor(rest[:, :, :], rest[:, :, :], b2[:, :, 1, :], ALU.subtract))
        c.link(dve.tensor_copy(b2[:, :, 2, :], rest[:, :, :]))
        return dve.tensor_tensor(sb2[:, :], w["L1f_sb2"][:, 0:1], w["L1f_sb2"][:, 1:2], ALU.add)

    def router(core, stage, T):
        r = SoftmaxRouter(core, stage, T, w["L1f_router"][:, :], w["L1f_router_b"][:, :])
        r.extra_down = [(b2[:, h, q, :], h) for h in range(2) for q in range(3)]
        return r

    ffn_stage(nc, core, "L1f", items, down, dict(post=1, pre=4, statistics=0, normalise=0, logits=6, exp=6,
              route=5, pieces=1, experts=15), core.loaded("L1f"), prepare=prepare, router=router, final_bias=sb2[:, :])


def ffn2(nc, core):
    w = core.w
    items = [Item(128, ACT.Silu, k % 3, gate=w["L2f_w1"][:, 128 * k:128 * k + 128],
                  up=w["L2f_w3"][:, 128 * k:128 * k + 128], expert=(w["L2f_select"][:, k, :], 0)) for k in range(12)]
    items.append(Item(96, ACT.Silu, 0, gate=w["L2f_w1"][:, 1536:1632], up=w["L2f_w3"][:, 1536:1632]))
    down = [(w["L2f_w2"][:, k, :], k) for k in range(12)] + [(w["L2f_ws2"][:, :], 12)]
    ffn_stage(nc, core, "L2f", items, down, dict(post=1, pre=3, statistics=0, normalise=0, logits=4, exp=4,
              route=4, pieces=2, experts=12), core.loaded("L2f"),
              router=lambda core, stage, T: GroupRouter(core, stage, T, w["L2f_router"][:, :], w["L2f_router_b"][:, :]))


def ffn3(nc, core):
    w = core.w
    items = [Item(128, ACT.Silu, k, gate=w["L3f_w1"][:, 128 * k:128 * k + 128],
                  up=w["L3f_w2"][:, 128 * k:128 * k + 128], scale=w["L3f_w1_s"][:, k:k + 1],
                  up_scale=w["L3f_w2_s"][:, k:k + 1]) for k in range(4)]
    for layer, name in ((1, "h1"), (2, "h2")):
        items += [Item(128, ACT.Gelu, 4 * layer + k, scale=w[f"L3f_{name}_s"][:, k:k + 1],
                       deep=[(w[f"L3f_{name}"][:, j, 128 * k:128 * k + 128], 4 * layer - 4 + j) for j in range(4)])
                  for k in range(4)]
    ffn_stage(nc, core, "L3f", items, [(w["L3f_w3"][:, k, :], 8 + k) for k in range(4)],
              dict(post=1, pre=4, statistics=0, normalise=3), core.loaded("L3f"), final_scale=w["L3f_w3_s"][:, :])


STAGES = {"L0a": attention0, "L0f": ffn0, "L1a": landmark_attention, "L1f": ffn1,
          "L2a": lambda nc, core: rope_attention(nc, core, "L2a"), "L2f": ffn2,
          "L3a": lambda nc, core: rope_attention(nc, core, "L3a"), "L3f": ffn3}
ORDER = ("L0a", "L0f", "L1a", "L1f", "L2a", "L2f", "L3a", "L3f")


def sandwich_kernel(nc, x, out, given, stages=ORDER):
    with ExitStack() as ctx:
        core = Core(nc, ctx)
        core.ident = core.sbuf("ident", [128, 128])
        core.ident16 = core.sbuf("ident16", [128, 128], BF16)
        core.weights = Weights(core, ctx, given, stages)
        core.w, core.loaded = core.weights.views, core.weights.loaded
        core.x_loaded, constants, ident16_made, core.stored = (
            ctx.enter_context(nc.semaphore(n)) for n in ("x_loaded", "constants", "ident16_made", "stored"))
        core.out = out.rearrange("b (h p) f -> p (b h) f", p=128)


        with nc.Block() as block:
            @block.sync
            def _(sp):
                rows = x.rearrange("b (h p) f -> p (b h) f", p=128)
                sp.dma_start(core.x[:, 0:FFN_TILES, :], rows[:, 0:FFN_TILES, :]).then_inc(core.x_loaded, 16)
                sp.dma_start(core.ident[:, :], given["ident"]).then_inc(constants, 16)
                core.weights.load(sp, stages[0])
                sp.dma_start(core.x[:, FFN_TILES:TILES, :], rows[:, FFN_TILES:, :]).then_inc(core.x_loaded, 16)
                for s in stages[1:2]:
                    core.weights.load(sp, s)
                sp.wait_ge(constants, 16)

            @block.gpsimd
            def _(pool):
                pool.memset(core.half[:, :], -0.5)
                pool.memset(core.x[:, TILES:, :], 0.0)
                pool.memset(core.eps[:, :], EPS)
                pool.memset(core.zero[:, :], 0.0)
                pool.dma_start(core.ident16[:, :], given["ident"]).then_inc(ident16_made, 16)
                for s in stages[:2]:
                    core.weights.load_converted(pool, s)
                pool.wait_ge(ident16_made, 16)

        for s in stages:
            STAGES[s](nc, core)


def kernel(**inputs):
    import numpy as _np
    import concourse.bacc as _bacc
    from concourse import mybir as _mybir
    from concourse.bass_utils import run_bass_kernel_spmd as _run

    nc = _bacc.Bacc("TRN2", target_bir_lowering=False, num_devices=1)
    given = {k: _np.asarray(v) for k, v in inputs.items()}
    arrays = {"x": _np.ascontiguousarray(given["L0_attn_x"]), **lay_out(given)}
    aps = {n: nc.dram_tensor(f"in_{n}", v.shape, _mybir.dt.from_np(v.dtype), kind="ExternalInput").ap()
           for n, v in arrays.items()}
    out = nc.dram_tensor("out_0", arrays["x"].shape, _mybir.dt.float32, kind="ExternalOutput").ap()
    sandwich_kernel(nc, aps.pop("x"), out, aps)
    r = _run(nc, [{f"in_{n}": v for n, v in arrays.items()}], core_ids=[0])
    return r.results[0]["out_0"]
```
